# Optimizing a Trainium2 kernel written in Bass

```python
import numpy as np
import jax
import jax.numpy as jnp

def _softmax(x, axis=-1):
    return jax.nn.softmax(x, axis=axis)

def _gelu(x):
    return jax.nn.gelu(x, approximate=True)

def _silu(x):
    return jax.nn.silu(x)

def _sigmoid(x):
    return jax.nn.sigmoid(x)

def _layernorm(x, axis=-1, eps=1e-05):
    m = jnp.mean(x, axis=axis, keepdims=True)
    v = jnp.var(x, axis=axis, keepdims=True)
    return (x - m) / jnp.sqrt(v + eps)

def _scatter_add(tgt, idx, src, axis=0):
    return tgt.at[idx].add(src)

def _segment_sum(src, seg, n):
    return jax.ops.segment_sum(src, seg, n)
kernel_name = 'mk_cond_resid_d4_seqx_r2_8e0f27'

def setup_inputs(seed: int=0):
    np.random.seed(seed)
    _w = jnp.asarray

    def _rec_inputs():
        import jax
        import jax.numpy as jnp
        _rk = jax.random.key(seed)
        x = -7.109e-05 + 0.9999 * jax.random.normal(jax.random.fold_in(_rk, 1), (4, 1024, 512), jnp.float32)
        _lenS = 1024 - jax.random.randint(jax.random.fold_in(_rk, 7), (4,), 0, max(1, 1024 // 4) + 1, jnp.int32)
        _lenS2 = 1024 - jax.random.randint(jax.random.fold_in(_rk, 8), (4,), 0, max(1, 1024 // 4) + 1, jnp.int32)
        cond_1024 = 0.00191187 + 0.999416 * jax.random.normal(jax.random.fold_in(_rk, 11), (4, 512), jnp.float32)
        return (x, cond_1024)
    x, cond_1024 = _rec_inputs()

    def _L0_cond_setup():
        import jax, jax.numpy as jnp
        import numpy as np
        N, T, D, H = (128, 128, 512, 512)
        key = jax.random.key(seed)
        k1, k2, k3, k4 = jax.random.split(key, 4)
        x = jax.random.normal(k1, (N, T, D), dtype=jnp.float32)
        h0 = jax.random.normal(k2, (N, H), dtype=jnp.float32)
        Wx = jax.random.normal(k3, (D, H), dtype=jnp.float32) / jnp.sqrt(jnp.float32(D))
        Wh = jax.random.normal(k4, (H, H), dtype=jnp.float32) / jnp.sqrt(jnp.float32(H))
        b = jnp.zeros((H,), dtype=jnp.float32)
        return {'x': x, 'h0': h0, 'Wx': Wx, 'Wh': Wh, 'b': b}
    _L0_cond_all = _L0_cond_setup()
    _L0_cond_in = {k: v for k, v in _L0_cond_all.items() if k in ('Wx', 'Wh', 'b')}
    del _L0_cond_all

    def _L1_cond_setup():
        import jax, jax.numpy as jnp
        import numpy as np
        key = jax.random.key(seed)
        ks = jax.random.split(key, 8)
        B, L, D, N, K = (4, 2048, 512, 64, 4)
        return {'x': jax.random.normal(ks[0], (B, L, D), dtype=jnp.float32), 'conv_w': jax.random.normal(ks[1], (K, 1, D), dtype=jnp.float32) * 0.1, 'conv_b': jnp.zeros((D,), dtype=jnp.float32), 'Wp': jax.random.normal(ks[2], (D, 2 * N), dtype=jnp.float32) * (1.0 / np.sqrt(D)), 'bp': jnp.zeros((2 * N,), dtype=jnp.float32), 'Ws': jax.random.normal(ks[3], (D, N), dtype=jnp.float32) * (1.0 / np.sqrt(D)), 'bs': jnp.zeros((N,), dtype=jnp.float32), 'A_log': jax.random.normal(ks[4], (N,), dtype=jnp.float32) * 0.02, 'dt_log': jax.random.normal(ks[5], (N,), dtype=jnp.float32) * 0.02, 'Wo': jax.random.normal(ks[6], (N, D), dtype=jnp.float32) * (1.0 / np.sqrt(N)), 'bo': jnp.zeros((D,), dtype=jnp.float32)}
    _L1_cond_all = _L1_cond_setup()
    _L1_cond_in = {k: v for k, v in _L1_cond_all.items() if k in ('conv_b', 'Wp', 'bp', 'Ws', 'bs', 'A_log', 'dt_log', 'Wo', 'bo')}
    del _L1_cond_all

    def _L2_cond_setup():
        import jax, jax.numpy as jnp
        import numpy as np
        N, T, D, H = (64, 256, 512, 512)
        key = jax.random.key(seed)
        k1, k2, k3, k4 = jax.random.split(key, 4)
        x = jax.random.normal(k1, (N, T, D), dtype=jnp.float32)
        h0 = jax.random.normal(k2, (N, H), dtype=jnp.float32)
        Wx = jax.random.normal(k3, (D, 4 * H), dtype=jnp.float32) / np.sqrt(D)
        Wh = jax.random.normal(k4, (H, 4 * H), dtype=jnp.float32) / np.sqrt(H)
        b = jnp.zeros((4 * H,), dtype=jnp.float32)
        return {'x': x, 'h0': h0, 'Wx': Wx, 'Wh': Wh, 'b': b}
    _L2_cond_all = _L2_cond_setup()
    _L2_cond_in = {k: v for k, v in _L2_cond_all.items() if k in ('Wx', 'Wh', 'b')}
    del _L2_cond_all

    def _L3_cond_setup():
        import jax, jax.numpy as jnp
        import numpy as np
        B, T, D = (128, 32, 512)
        ADA, INTER, RANK = (512, 512, 8)
        LN_EPS = 1e-05

        def _layernorm(x, g, b):
            mu = jnp.mean(x, axis=-1, keepdims=True)
            var = jnp.var(x, axis=-1, keepdims=True)
            return (x - mu) * jax.lax.rsqrt(var + LN_EPS) * g + b
        key = jax.random.key(seed)
        ks = jax.random.split(key, 9)
        return {'x': jax.random.normal(ks[0], (B, T, D), dtype=jnp.float32), 'ada_emb': jax.random.normal(ks[1], (B, ADA), dtype=jnp.float32), 'base_layer': jax.random.normal(ks[2], (D, D), dtype=jnp.float32), 'w1': jax.random.normal(ks[3], (ADA, INTER), dtype=jnp.float32) * 0.02, 'b1': jnp.zeros((INTER,), dtype=jnp.float32), 'w2': jax.random.normal(ks[4], (INTER, 2 * D * RANK), dtype=jnp.float32) * 0.02, 'b2': jnp.zeros((2 * D * RANK,), dtype=jnp.float32), 'ln_g': jnp.ones((ADA,), dtype=jnp.float32), 'ln_b': jnp.zeros((ADA,), dtype=jnp.float32)}
    _L3_cond_all = _L3_cond_setup()
    _L3_cond_in = {k: v for k, v in _L3_cond_all.items() if k in ('base_layer', 'w1', 'b1', 'w2', 'b2', 'ln_g', 'ln_b')}
    del _L3_cond_all
    return {'x': x, 'cond_1024': cond_1024, 'L0_cond_Wx': _L0_cond_in['Wx'], 'L0_cond_Wh': _L0_cond_in['Wh'], 'L0_cond_b': _L0_cond_in['b'], 'L1_cond_conv_b': _L1_cond_in['conv_b'], 'L1_cond_Wp': _L1_cond_in['Wp'], 'L1_cond_bp': _L1_cond_in['bp'], 'L1_cond_Ws': _L1_cond_in['Ws'], 'L1_cond_bs': _L1_cond_in['bs'], 'L1_cond_A_log': _L1_cond_in['A_log'], 'L1_cond_dt_log': _L1_cond_in['dt_log'], 'L1_cond_Wo': _L1_cond_in['Wo'], 'L1_cond_bo': _L1_cond_in['bo'], 'L2_cond_Wx': _L2_cond_in['Wx'], 'L2_cond_Wh': _L2_cond_in['Wh'], 'L2_cond_b': _L2_cond_in['b'], 'L3_cond_base_layer': _L3_cond_in['base_layer'], 'L3_cond_w1': _L3_cond_in['w1'], 'L3_cond_b1': _L3_cond_in['b1'], 'L3_cond_w2': _L3_cond_in['w2'], 'L3_cond_b2': _L3_cond_in['b2'], 'L3_cond_ln_g': _L3_cond_in['ln_g'], 'L3_cond_ln_b': _L3_cond_in['ln_b']}

def reference(x, cond_1024, L0_cond_Wx, L0_cond_Wh, L0_cond_b, L1_cond_conv_b, L1_cond_Wp, L1_cond_bp, L1_cond_Ws, L1_cond_bs, L1_cond_A_log, L1_cond_dt_log, L1_cond_Wo, L1_cond_bo, L2_cond_Wx, L2_cond_Wh, L2_cond_b, L3_cond_base_layer, L3_cond_w1, L3_cond_b1, L3_cond_w2, L3_cond_b2, L3_cond_ln_g, L3_cond_ln_b):
    import jax
    import jax.numpy as jnp

    def _L0_cond_ref(x, h0, Wx, Wh, b):
        import jax, jax.numpy as jnp
        import numpy as np
        N, T, D, H = (128, 128, 512, 512)
        xW = jnp.einsum('ntd,dh->nth', x, Wx) + b

        def step(prev_h, xw_t):
            next_h = jnp.tanh(xw_t + prev_h @ Wh)
            return (next_h, next_h)
        _, hs = jax.lax.scan(step, h0, jnp.swapaxes(xW, 0, 1))
        return jnp.swapaxes(hs, 0, 1)

    def _L1_cond_ref(x, conv_w, conv_b, Wp, bp, Ws, bs, A_log, dt_log, Wo, bo):
        import jax, jax.numpy as jnp
        import numpy as np
        B, L, D = x.shape
        K = conv_w.shape[0]
        N = Ws.shape[1]
        x_pad = jnp.pad(x, ((0, 0), (K - 1, 0), (0, 0)))
        conv = conv_b + sum((x_pad[:, k:k + L, :] * conv_w[k, 0] for k in range(K)))
        proj = conv @ Wp + bp
        B_t = jax.nn.softplus(proj[..., :N])
        C_t = jnp.tanh(proj[..., N:])
        u = x @ Ws + bs
        A = -jax.nn.softplus(A_log)
        dt = jax.nn.softplus(dt_log)
        decay = 1.0 + dt * A

        def step(state, inputs):
            u_t, b_t, c_t = inputs
            state = decay * state + dt * b_t * u_t
            return (state, c_t * state)
        init = jnp.zeros((B, N), dtype=x.dtype)
        xs = tuple((jnp.swapaxes(a, 0, 1) for a in (u, B_t, C_t)))
        _, ys = jax.lax.scan(step, init, xs, unroll=4)
        y = jnp.swapaxes(ys, 0, 1)
        return y @ Wo + bo

    def _L2_cond_ref(x, h0, Wx, Wh, b):
        import jax, jax.numpy as jnp
        import numpy as np
        N, T, D, H = (64, 256, 512, 512)
        Hdim = h0.shape[1]
        xW = jnp.einsum('ntd,dg->ntg', x, Wx) + b
        c0 = jnp.zeros_like(h0)

        def step(carry, xw_t):
            prev_h, prev_c = carry
            A = xw_t + prev_h @ Wh
            i = jax.nn.sigmoid(A[:, 0:Hdim])
            f = jax.nn.sigmoid(A[:, Hdim:2 * Hdim])
            o = jax.nn.sigmoid(A[:, 2 * Hdim:3 * Hdim])
            g = jnp.tanh(A[:, 3 * Hdim:4 * Hdim])
            next_c = f * prev_c + i * g
            next_h = o * jnp.tanh(next_c)
            return ((next_h, next_c), next_h)
        _, hs = jax.lax.scan(step, (h0, c0), jnp.swapaxes(xW, 0, 1))
        return jnp.swapaxes(hs, 0, 1)

    def _L3_cond_ref(x, ada_emb, base_layer, w1, b1, w2, b2, ln_g, ln_b):
        import jax, jax.numpy as jnp
        import numpy as np
        B, T, D = (128, 32, 512)
        ADA, INTER, RANK = (512, 512, 8)
        LN_EPS = 1e-05

        def _layernorm(x, g, b):
            mu = jnp.mean(x, axis=-1, keepdims=True)
            var = jnp.var(x, axis=-1, keepdims=True)
            return (x - mu) * jax.lax.rsqrt(var + LN_EPS) * g + b
        b, t, d = x.shape
        ae = _layernorm(ada_emb, ln_g, ln_b)
        h = jax.nn.gelu(ae @ w1 + b1, approximate=False)
        xw = h @ w2 + b2
        x_a, x_b = jnp.split(xw, 2, axis=-1)
        x_a = x_a.reshape(b, d, RANK)
        x_b = x_b.reshape(b, d, RANK)
        layer = base_layer[None, :, :] + jnp.einsum('bdr,bkr->bdk', x_a, x_b)
        out = jnp.einsum('btc,bco->bto', x, layer)
        return x + out
    x = x + _L0_cond_ref(x, cond_1024, L0_cond_Wx, L0_cond_Wh, L0_cond_b)
    x = x + _L1_cond_ref(x, cond_1024[:, None, :], L1_cond_conv_b, L1_cond_Wp, L1_cond_bp, L1_cond_Ws, L1_cond_bs, L1_cond_A_log, L1_cond_dt_log, L1_cond_Wo, L1_cond_bo)
    x = x + _L2_cond_ref(x, cond_1024, L2_cond_Wx, L2_cond_Wh, L2_cond_b)
    x = x + _L3_cond_ref(x, cond_1024, L3_cond_base_layer, L3_cond_w1, L3_cond_b1, L3_cond_w2, L3_cond_b2, L3_cond_ln_g, L3_cond_ln_b)
    return x

_drawn_inputs = setup_inputs


def setup_inputs(seed=0):
    import zlib

    import numpy as np

    out = dict(_drawn_inputs(seed))
    spreads = {'L0_cond_b': (0.0, 0.1),
     'L1_cond_conv_b': (0.0, 0.1),
     'L1_cond_bp': (0.0, 0.1),
     'L1_cond_bs': (0.0, 0.1),
     'L1_cond_bo': (0.0, 0.1),
     'L2_cond_b': (0.0, 0.551),
     'L3_cond_b1': (0.0, 0.513),
     'L3_cond_b2': (0.0, 0.1),
     'L3_cond_ln_g': (1.0, 0.6),
     'L3_cond_ln_b': (0.0, 0.8)}
    factors = {'L1_cond_A_log': 7.019, 'L1_cond_dt_log': 4.992}
    for name, (base, spread) in spreads.items():
        noise = np.random.default_rng([zlib.crc32(name.encode()), seed]).standard_normal(out[name].shape)
        drawn = base * np.exp(spread * noise) if base else spread * noise
        out[name] = jnp.asarray(drawn.astype(out[name].dtype))
    for name, factor in factors.items():
        out[name] = (out[name] * factor).astype(out[name].dtype)
    return out
```

```python
import numpy as np
import concourse.bass as bass
from concourse import mybir
from contextlib import ExitStack

F32 = mybir.dt.float32
F16 = mybir.dt.float16
U32 = mybir.dt.uint32
ALU = mybir.AluOpType
ACT = mybir.ActivationFunctionType
AX = mybir.AxisListType
RMAX = bass.bass_isa.ReduceOp.max

P = 128
NB, T, D = 4, 1024, 512
CT = 32
NCH = T // CT
TOK = NB * CT
KB = D // P
QC = 32
NQ = P // QC
G = 4
GB = G * KB
NS = 64
TAPS = 4
RANK = 8
LN_EPS = 1e-5
H_SCALE = 4096.0
R_SCALE = 8192.0
PIECE = 8
W2C = 1024
W2R = 2 * D * RANK // W2C
DP = W2C // NQ // RANK

XT_STEP = 1
SSM_STEP = 4
L0_STEP = 7
SOFT_STEP = 7
WO_STEP = 12
L2_STEP = 14
L2_MM = 6
L2_ALL = GB * KB


def l2_last_step(g):
    return L2_STEP + (KB * KB * (g + 1) - 1) // L2_MM


def chunk_work(i):
    return dict(rnn=0 <= i < NCH, l0=i + 1 < NCH, mid=1 <= i <= NCH, lstm=2 <= i <= NCH + 1, out=3 <= i <= NCH + 2)


FIRST_FULL, LAST_FULL = 3, NCH - 2
HEAD = list(range(0, FIRST_FULL))
TAIL = list(range(LAST_FULL + 1, NCH + 3))


def resid_stack_kernel(nc, x, cond, l0_Wx, l0_Wh, l0_b, conv_b, Wp, bp, Ws, bs, A_log, dt_log, Wo, bo,
                       l2_Wx, l2_Wh, l2_b, base, w1, b1, w2, b2, ln_g, ln_b, out):
    ctx = ExitStack()
    with ctx:
        def sb(name, shape, dt=F32):
            return ctx.enter_context(nc.sbuf_tensor(name, shape, dt))

        def pb(name):
            return ctx.enter_context(nc.psum_tensor(name, [P, 512], F32))

        def sem(name):
            return ctx.enter_context(nc.semaphore(name))

        stage = sb("stage", [P, 5 * 2048])

        def reuse(at):
            return stage[:, at * KB * TOK:(at + 1) * KB * TOK]

        whl = sb("lstm_Wh_parts", [P, KB, 2, NQ, G * P], F16)
        whr = sb("rnn_Wh_parts", [P, KB, 2, KB, P], F16)
        wxl = sb("lstm_Wx", [P, KB, G * D])
        wxr = sb("rnn_Wx", [P, KB, D])
        wp = sb("ssm_Wp", [P, KB, 2 * NS])
        ws = sb("ssm_Ws", [P, KB, NS])
        wo = sb("ssm_Wo", [NS, D])
        layer = sb("layer_plus_2I", [P, NB, KB, D])
        condT = sb("condT", [P, KB, NB])
        b_rnn = sb("b_rnn", [P, KB])
        b_lstm = sb("b_lstm", [P, GB])
        b_conv = sb("b_conv", [P, KB])
        b_out = sb("b_ssm_out", [P, KB])
        b_B = sb("b_B", [NS, 1])
        b_C = sb("b_C", [NS, 1])
        b_u = sb("b_u", [NS, 1])
        ab = sb("A_dt_log", [NS, 2])
        spt = sb("softplus_A_dt", [NS, 2])
        decay = sb("decay", [NS, CT])
        decay1 = sb("decay1", [NS, 1])
        ident = sb("ident", [P, P])
        wmax = sb("wmax", [P, 2])
        wmaxa = sb("wmaxa", [P, 2])
        wpow = sb("wpow", [P, 2])
        wscale = sb("wscale", [P, 2])
        unscale = sb("unscale", [P, 2])
        h0r = sb("h0_rnn", [P, KB, NB])
        h0l = sb("h0_lstm", [P, GB, NB])
        xrow = sb("x_rows", [P, D])
        xT_nxt = reuse(0).rearrange("p (b t n) -> p b t n", b=KB, t=CT)
        xT_cur = sb("xT_cur", [P, KB, CT, NB])
        xr_nxt = reuse(1).rearrange("p (b t n) -> p b t n", b=KB, t=CT)
        xr_cur = sb("rnn_in_cur", [P, KB, CT, NB])
        hr = sb("rnn_h", [P, KB, CT, NB])
        HALO = TAPS - 1
        x1T = sb("x1T", [P, KB, HALO + CT, NB])
        x2_nxt = sb("x2_nxt", [P, KB, CT, NB])
        x2_cur = sb("x2_cur", [P, KB, CT, NB])
        xl_nxt = sb("lstm_in_nxt", [P, CT, GB, NB])
        xl_cur = sb("lstm_in_cur", [P, CT, GB, NB])
        hl = sb("lstm_h_scaled", [P, KB, CT, NB])
        x3T = sb("x3T", [P, KB, CT, NB])
        orow = sb("out_rows", [P, D])
        hrs = sb("rnn_h_parts", [P, KB, 2, NB], F16)
        hls = sb("lstm_h_parts", [P, KB, 2, NB], F16)
        r_s1 = sb("rnn_sum1", [P, KB, NB])
        r_s2 = sb("rnn_sum2", [P, KB, NB])
        tr = reuse(2).rearrange("p (g r) -> p g r", g=GB)
        l_s1 = sb("lstm_sum1", [P, GB, NB])
        l_s2 = sb("lstm_sum2", [P, GB, NB])
        gate = sb("lstm_gates", [P, G, KB * NB])
        cell = sb("lstm_2c", [P, KB * NB])
        c_f = sb("lstm_f_part", [P, KB * NB])
        c_i = sb("lstm_i_part", [P, KB * NB])
        o_s = sb("lstm_o_scaled", [P, KB * NB])
        tc = sb("lstm_tanh_c", [P, KB * NB])
        conv = reuse(3).rearrange("p (b t n) -> p b t n", b=KB, t=CT)
        zabs = sb("zabs", [NS, TOK])
        zmax = sb("zmax", [NS, TOK])
        ez = sb("ez", [NS, TOK])
        den = sb("den", [NS, TOK])
        rden = sb("rden", [NS, TOK])
        sr = sb("sr", [NS, TOK])
        qr = sb("qr", [NS, TOK])
        pol = sb("pol", [NS, 2, TOK])
        bt = sb("B_t", [NS, TOK])
        ct = sb("C_t", [NS, TOK])
        drive = sb("drive", [NS, TOK])
        states = sb("states", [NS, CT, NB])
        st0 = sb("state0", [NS, NB])
        y = sb("y", [NS, TOK])
        whl32 = stage[:, 0:8192].rearrange("p (k n) -> p k n", k=KB)
        whr32 = stage[:, 8192:10240].rearrange("p (k n) -> p k n", k=KB)
        w1s = whr32
        w2s = [stage[:, h * 4096:(h + 1) * 4096].rearrange("p (k n) -> p k n", k=KB) for h in range(2)]
        b2s = xl_nxt[:, :, :, :].rearrange("p t g n -> p (t g n)").rearrange("p (q n) -> p q n", q=W2R)
        xw = xl_cur[:, :, :, :].rearrange("p t g n -> p (t g n)").rearrange("p (q r d) -> p q r d", q=W2R, r=RANK)
        xab = stage[0:RANK, 8192:10240].rearrange("p (n d) -> p n d", n=NB)
        xbb = stage[0:RANK, 0:2048].rearrange("p (n d) -> p n d", n=NB)
        baseI = layer[:, NB - 1, :, :]
        ae = orow[0:NB, :]
        crow, lng, lnb, lnc, lnq = [t[0:NB, :, :, :].rearrange("p b t n -> p (b t n)") for t in (x2_nxt, x2_cur, x3T, hl, hr)]
        stat = sb("ln_stat", [NB, 8])
        aeT = sb("aeT", [P, KB, NB])
        hmT = sb("hmT", [P, KB, NB])
        b1T = sb("b1T", [P, KB])

        psL, psR, psOut, psX, psS, psI, psA, psB = [pb(n) for n in
            ("ps_lstm", "ps_rnn", "ps_out", "ps_x", "ps_ssm", "ps_rnn_in", "ps_lstm_in_a", "ps_lstm_in_b")]
        ps_rnn = psR[:, 0:KB * 2 * NB].rearrange("p (m s n) -> p m s n", m=KB, s=2)

        d_rnnw, d_x0, d_lstmw, d_small, d_w1, d_w2a, d_w2b, d_xab, d_ln = [sem(n) for n in
            ("d_rnnw", "d_x0", "d_lstmw", "d_small", "d_w1", "d_w2a", "d_w2b", "d_xab", "d_ln")]
        d_w2 = [d_w2a, d_w2b]
        q_id, q_zero, q_vec, q_pool, q_pe, q_act = [sem(n) for n in
            ("q_id", "q_zero", "q_vec", "q_pool", "q_pe", "q_act")]
        arrive = sem("engines_arrived")
        go = {e: sem(f"go_{e}") for e in ("pe", "act", "vec", "pool")}
        names = ["lstm_mm", "lstm_summed", "lstm_gated", "lstm_cell", "lstm_tanhc", "lstm_h_ready",
                 "rnn_mm", "rnn_summed", "rnn_tanh", "rnn_h_ready", "vec_done", "pool_done",
                 "x_arrived", "xT_mm", "xT_ready", "l0_mm", "l0_ready",
                 "conv_ready", "ssm_mm", "zabs_ready", "exp_ready", "c_ready", "y_ready", "wo_mm",
                 "x2_ready", "l2_mm", "l2_ready", "out_mm", "out_ready", "out_stored"]
        S = {n: sem(n) for n in names}
        nums = sorted(s.num for s in S.values())
        assert nums == list(range(nums[0], nums[0] + len(nums)))
        chunk_sems = range(nums[0], nums[-1] + 1)

        block = ctx.enter_context(nc.Block())

        def rows(w):
            return w.rearrange("(k p) n -> p k n", p=P)

        def column(v):
            return v.rearrange("(k p) -> p k", p=P)

        def pipeline(eng, body):
            for i in HEAD:
                body(i, i, chunk_work(i))
            with eng.Fori(FIRST_FULL, LAST_FULL + 1) as i:
                body(i, None, chunk_work(FIRST_FULL))
            for i in TAIL:
                body(i, i, chunk_work(i))

        def meet(eng, name):
            eng.drain().then_inc(arrive, 1)
            eng.wait_ge(go[name], 1)
            eng.sem_clear(go[name])

        @block.sync
        def _(sp):
            x_v = x.rearrange("n (i t) d -> i n t d", t=CT)
            out_v = out.rearrange("n (i t) d -> i n t d", t=CT)
            with nc.allow_non_contiguous_dma("weights in hidden layout"):
                sp.dma_start(whr32, rows(l0_Wh)).then_inc(d_rnnw, 16)
                sp.dma_start(wxr[:, :, :], rows(l0_Wx)).then_inc(d_rnnw, 16)
                for n in range(NB):
                    sp.dma_start(condT[:, :, n], column(cond[n])).then_inc(d_rnnw, 16)
                sp.dma_start(b_rnn[:, :], column(l0_b)).then_inc(d_rnnw, 16)
                sp.dma_start(xrow[:, :], x_v[0]).then_inc(d_x0, 16)
                sp.dma_start(whl32, rows(l2_Wh)).then_inc(d_lstmw, 16)
                cut = lambda v, a: v[a:a + NS].rearrange("(p o) -> p o", o=1)
                for dst, src in ((b_lstm[:, :], column(l2_b)), (b_conv[:, :], column(conv_b)), (b_out[:, :], column(bo)),
                                 (b_B[:, :], cut(bp, 0)), (b_C[:, :], cut(bp, NS)), (b_u[:, :], cut(bs, 0)),
                                 (ab[:, 0:1], cut(A_log, 0)), (ab[:, 1:2], cut(dt_log, 0)),
                                 (wp[:, :, :], rows(Wp)), (ws[:, :, :], rows(Ws)), (wo[:, :], Wo[:, :]),
                                 (wxl[:, :, :], rows(l2_Wx)), (baseI, rows(base))):
                    sp.dma_start(dst, src).then_inc(d_small, 16)
                row = lambda v: v.rearrange("(o n) -> o n", o=1)
                sp.dma_start(crow[:, :], cond[:, :]).then_inc(d_ln, 16)
                for n in range(NB):
                    sp.dma_start(lng[n:n + 1, :], row(ln_g)).then_inc(d_ln, 16)
                    sp.dma_start(lnb[n:n + 1, :], row(ln_b)).then_inc(d_ln, 16)
                    for q in range(NQ):
                        src = b2.rearrange("(a q g d) -> a q g d", a=1, g=NQ, d=W2C // NQ)[:, :, q, :]
                        sp.dma_start(b2s[QC * q + n:QC * q + n + 1, :, :], src).then_inc(d_ln, 16)
                sp.dma_start(b1T[:, :], column(b1)).then_inc(d_ln, 16)
                sp.wait_ge(q_vec, V_SPLIT)
                sp.wait_ge(q_pe, PE_H0)
                sp.dma_start(w1s, rows(w1)).then_inc(d_w1, 16)
                w2v = w2.rearrange("(k p) (q n) -> q p k n", p=P, n=W2C)
                for q in range(W2R):
                    if q >= 2:
                        sp.wait_ge(q_pe, PE_W2 + q - 1)
                    sp.dma_start(w2s[q % 2], w2v[q]).then_inc(d_w2[q % 2], 16)
                sp.wait_ge(q_vec, V_XW)
                for half, dst in ((0, xab), (1, xbb)):
                    for q in range(NQ):
                        for n in range(NB):
                            for a in range(W2R // 2):
                                f = P * a + DP * q
                                sp.dma_start(dst[:, n, f:f + DP], xw[QC * q + n:QC * q + n + 1, half * (W2R // 2) + a, :, :]
                                             ).then_inc(d_xab, 16)

            def body(i, _known, w):
                if w["l0"]:
                    sp.dma_start(xrow[:, :], x_v[i + 1]).then_inc(S["x_arrived"], 16)
                if w["out"]:
                    sp.wait_ge(S["out_ready"], 1)
                    for n in range(NB):
                        sp.dma_start(out_v[i - 3, n], orow[CT * n:CT * (n + 1), :]).then_inc(S["out_stored"], 16)
                    sp.wait_ge(S["out_stored"], 16 * NB)
                sp.wait_ge(arrive, 4)
                sp.sem_clear(chunk_sems)
                sp.sem_clear(arrive)
                for e in go.values():
                    sp.sem_inc(e, 1)

            sp.wait_ge(arrive, 4)
            sp.sem_clear(arrive)
            for e in go.values():
                sp.sem_inc(e, 1)
            pipeline(sp, body)

        @block.gpsimd
        def _(pool):
            nc.gpsimd.memset(ident[:, :], 0.0).then_inc(q_id, 1)
            pool.wait_ge(q_id, 1)
            nc.gpsimd.affine_select(out=ident[:, :], in_=ident[:, :], compare_op=ALU.not_equal, fill=1.0, base=0,
                                    pattern=[[-1, P]], channel_multiplier=1).then_inc(q_id, 1)
            pool.wait_ge(q_vec, 1)
            nc.gpsimd.partition_all_reduce(wmaxa[:, 0:1], wmax[:, 0:1], P, RMAX).then_inc(q_pool, 1)
            pool.wait_ge(q_vec, V_LMAX)
            nc.gpsimd.partition_all_reduce(wmaxa[:, 1:2], wmax[:, 1:2], P, RMAX).then_inc(q_pool, 1)
            meet(pool, "pool")

            def body(_i, _known, w):
                n = [0]

                def step(ins):
                    n[0] += 1
                    ins.then_inc(S["pool_done"], 1)
                    pool.wait_ge(S["pool_done"], n[0])

                t0 = lambda q: slice(q * PIECE, (q + 1) * PIECE)
                halo_done = False
                for q in range(CT // PIECE):
                    if w["rnn"]:
                        pool.wait_ge(S["rnn_h_ready"], PIECE * (q + 1))
                        if w["mid"] and not halo_done:
                            pool.wait_ge(S["x2_ready"], KB)
                        if not halo_done:
                            step(nc.gpsimd.tensor_copy(x1T[:, :, 0:HALO, :], x1T[:, :, CT:CT + HALO, :]))
                            halo_done = True
                        step(nc.gpsimd.tensor_tensor(x1T[:, :, HALO + q * PIECE:HALO + (q + 1) * PIECE, :],
                                                     xT_cur[:, :, t0(q), :], hr[:, :, t0(q), :], ALU.add))
                    if w["l0"]:
                        if q == 0:
                            pool.wait_ge(S["l0_ready"], KB)
                        step(nc.gpsimd.tensor_copy(xT_cur[:, :, t0(q), :], xT_nxt[:, :, t0(q), :]))
                        step(nc.gpsimd.tensor_copy(xr_cur[:, :, t0(q), :], xr_nxt[:, :, t0(q), :]))
                    if w["lstm"]:
                        pool.wait_ge(S["lstm_h_ready"], PIECE * (q + 1))
                        if w["out"] and q == 0:
                            pool.wait_ge(S["out_mm"], 1)
                        step(nc.gpsimd.tensor_scalar(x3T[:, :, t0(q), :], hl[:, :, t0(q), :], 0.5 / H_SCALE, None, ALU.mult))
                        step(nc.gpsimd.tensor_tensor(x3T[:, :, t0(q), :], x3T[:, :, t0(q), :], x2_cur[:, :, t0(q), :], ALU.add))
                    if w["mid"]:
                        if q == 0:
                            pool.wait_ge(S["l2_ready"], GB)
                        step(nc.gpsimd.tensor_copy(x2_cur[:, :, t0(q), :], x2_nxt[:, :, t0(q), :]))
                        step(nc.gpsimd.tensor_copy(xl_cur[:, t0(q), :, :], xl_nxt[:, t0(q), :, :]))
                meet(pool, "pool")

            pipeline(pool, body)

        @block.scalar
        def _(act):
            act.wait_ge(q_pe, PE_X0)
            nc.scalar.activation(xT_cur[:, :, :, :].rearrange("p b t n -> p b n t"),
                                 psX[:, :].rearrange("p (b n t) -> p b n t", b=KB, n=NB), ACT.Identity).then_inc(q_act, 1)
            act.wait_ge(q_pe, PE_X0 + KB)
            for m in range(KB):
                nc.scalar.activation(xr_cur[:, m, :, :], psI[:, TOK * m:TOK * (m + 1)].rearrange("p (t n) -> p t n", n=NB),
                                     ACT.Identity, bias=b_rnn[:, m:m + 1]).then_inc(q_act, 1)
            act.wait_ge(d_small, 16 * 13)
            nc.scalar.activation(zabs[:, 0:2], ab[:, :], ACT.Abs).then_inc(q_act, 1)
            act.wait_ge(q_act, A_XR0 + 1)
            nc.scalar.activation(ez[:, 0:2], zabs[:, 0:2], ACT.Exp, scale=-1.0).then_inc(q_act, 1)
            act.wait_ge(q_vec, V_LNVAR)
            nc.scalar.activation(stat[:, 3:4], stat[:, 2:3], ACT.Sqrt).then_inc(q_act, 1)
            act.wait_ge(d_ln, 16 * (2 + NB * (2 + NQ)))
            act.wait_ge(q_pe, PE_W1 + KB)
            for m in range(KB):
                nc.scalar.activation(hmT[:, m, :], psB[:, NB * m:NB * (m + 1)], ACT.Gelu, bias=b1T[:, m:m + 1]).then_inc(q_act, 1)
            meet(act, "act")

            def body(_i, _known, w):
                for s in range(CT):
                    if w["lstm"]:
                        act.wait_ge(S["lstm_summed"], s + 1)
                        nc.scalar.activation(gate[:, :, :].rearrange("p g q -> p (g q)"),
                                             l_s2[:, :, :].rearrange("p g n -> p (g n)"), ACT.Tanh).then_inc(S["lstm_gated"], 1)
                    if w["rnn"]:
                        act.wait_ge(S["rnn_summed"], s + 1)
                        nc.scalar.activation(hr[:, :, s, :], r_s2[:, :, :], ACT.Tanh).then_inc(S["rnn_tanh"], 1)
                    if w["lstm"]:
                        act.wait_ge(S["lstm_cell"], s + 1)
                        nc.scalar.activation(tc[:, :], cell[:, :], ACT.Tanh, scale=0.5).then_inc(S["lstm_tanhc"], 1)
                    if w["l0"]:
                        if s == XT_STEP + 1:
                            act.wait_ge(S["xT_mm"], 1)
                            nc.scalar.activation(xT_nxt[:, :, :, :].rearrange("p b t n -> p b n t"),
                                                 psX[:, :].rearrange("p (b n t) -> p b n t", b=KB, n=NB),
                                                 ACT.Identity).then_inc(S["xT_ready"], 1)
                        if L0_STEP + KB <= s < L0_STEP + 2 * KB:
                            m = s - L0_STEP - KB
                            act.wait_ge(S["l0_mm"], KB)
                            nc.scalar.activation(xr_nxt[:, m, :, :],
                                                 psI[:, TOK * m:TOK * (m + 1)].rearrange("p (t n) -> p t n", n=NB),
                                                 ACT.Identity, bias=b_rnn[:, m:m + 1]).then_inc(S["l0_ready"], 1)
                    if w["mid"]:
                        if s == SOFT_STEP:
                            act.wait_ge(S["ssm_mm"], 1)
                            nc.scalar.activation(zabs[:, :], psS[0:NS, 0:TOK], ACT.Abs, bias=b_B[:, :]).then_inc(S["zabs_ready"], 1)
                            nc.scalar.activation(ct[:, :], psS[0:NS, TOK:2 * TOK], ACT.Tanh, bias=b_C[:, :]).then_inc(S["c_ready"], 1)
                            act.wait_ge(S["zabs_ready"], 1)
                            nc.scalar.activation(ez[:, :], zabs[:, :], ACT.Exp, scale=-1.0).then_inc(S["exp_ready"], 1)
                        for g in range(G):
                            if s == l2_last_step(g) + 1:
                                act.wait_ge(S["l2_mm"], g + 1)
                                ps = (psA, psB)[g % 2]
                                for b in range(KB):
                                    nc.scalar.activation(
                                        xl_nxt[:, :, g * KB + b, :],
                                        ps[:, TOK * b:TOK * (b + 1)].rearrange("p (t n) -> p t n", n=NB), ACT.Identity,
                                        bias=b_lstm[:, g * KB + b:g * KB + b + 1],
                                        scale=1.0 if g == G - 1 else 0.5).then_inc(S["l2_ready"], 1)
                meet(act, "act")

            pipeline(act, body)

        @block.vector
        def _(vec):
            n = [0]

            def prep(ins, wait=True):
                n[0] += 1
                ins.then_inc(q_vec, 1)
                if wait:
                    vec.wait_ge(q_vec, n[0])

            V = nc.vector
            vec.wait_ge(d_rnnw, 16 * (3 + NB))
            prep(V.tensor_reduce(wmax[:, 0:1], whr32.rearrange("p k n -> p (k n)"), AX.X, ALU.max, apply_absolute_value=True))
            vec.wait_ge(q_pool, 1)

            def scales(e, hs):
                prep(V.tensor_scalar(wpow[:, e:e + 1], wmaxa[:, e:e + 1], 1e-18, None, ALU.max))
                prep(V.tensor_scalar(wpow[:, e:e + 1].bitcast(U32), wpow[:, e:e + 1].bitcast(U32), 0x7F800000, None, ALU.bitwise_and))
                prep(V.tensor_scalar(wscale[:, e:e + 1].bitcast(U32), wpow[:, e:e + 1].bitcast(U32), 0x7F800000, None, ALU.bitwise_xor))
                prep(V.tensor_scalar(wscale[:, e:e + 1], wscale[:, e:e + 1], 4096.0, None, ALU.mult))
                prep(V.tensor_scalar(unscale[:, e:e + 1], wpow[:, e:e + 1], 0.5 / 4096.0 / hs, None, ALU.mult))

            scales(0, R_SCALE)
            for k in range(KB):
                for m in range(KB):
                    src = whr32[:, k, P * m:P * (m + 1)]
                    hi, lo = (whr[:, k, e, m, :] for e in range(2))
                    prep(V.tensor_scalar(hi, src, wscale[:, 0:1], None, ALU.mult))
                    prep(V.scalar_tensor_tensor(out=lo, in0=src, scalar=wscale[:, 0:1], in1=hi, op0=ALU.mult, op1=ALU.subtract))
            for t in (hrs[:, :, :, :], hls[:, :, :, :], cell[:, :], st0[:, :], x1T[:, :, :, :], psL[:, :]):
                prep(V.memset(t, 0.0))
            vec.wait_ge(d_lstmw, 16)
            prep(V.tensor_reduce(wmax[:, 1:2], whl32.rearrange("p k n -> p (k n)"), AX.X, ALU.max, apply_absolute_value=True))
            assert n[0] == V_LMAX, n[0]
            vec.wait_ge(q_pool, 2)
            scales(1, H_SCALE * 1.0)
            vec.wait_ge(q_pe, PE_H0)
            for k in range(KB):
                for g in range(G):
                    f = 0.5 if g < G - 1 else 1.0
                    f *= 0.5
                    src = whl32[:, k, g * D:(g + 1) * D].rearrange("p (b j c) -> p j b c", b=KB, j=NQ)
                    hi, lo = (whl[:, k, e, :, g * P:(g + 1) * P].rearrange("p j (b c) -> p j b c", b=KB) for e in range(2))
                    prep(V.tensor_scalar(src, src, wscale[:, 1:2], f, ALU.mult, ALU.mult))
                    prep(V.tensor_copy(hi, src))
                    prep(V.tensor_tensor(lo, src, hi, ALU.subtract))
            assert n[0] == V_SPLIT, n[0]
            prep(V.tensor_copy(h0r[:, :, :], psR[:, 0:KB * NB].rearrange("p (m n) -> p m n", n=NB)))
            for g in range(G):
                prep(V.tensor_scalar(h0l[:, g * KB:(g + 1) * KB, :],
                                     psR[:, 64 + g * KB * NB:64 + (g + 1) * KB * NB].rearrange("p (m n) -> p m n", n=NB),
                                     0.5 if g < G - 1 else 1.0, None, ALU.mult))
            vec.wait_ge(d_small, 16 * 13)
            prep(V.tensor_scalar(b_lstm[:, 0:(G - 1) * KB], b_lstm[:, 0:(G - 1) * KB], 0.5, None, ALU.mult))
            prep(V.tensor_scalar(zmax[:, 0:2], ab[:, :], 0.0, None, ALU.max))
            vec.wait_ge(q_act, A_EXP0)
            softplus(V, prep, zmax[:, 0:2], ez[:, 0:2], den[:, 0:2], rden[:, 0:2], sr[:, 0:2], qr[:, 0:2],
                     pol[:, 0, 0:2], pol[:, 1, 0:2], spt[:, :])
            prep(V.tensor_tensor(decay1[:, :], spt[:, 0:1], spt[:, 1:2], ALU.mult))
            prep(V.tensor_scalar(decay1[:, :], decay1[:, :], -1.0, 1.0, ALU.mult, ALU.add))
            prep(V.memset(decay[:, :], 1.0))
            prep(V.tensor_scalar(decay[:, :], decay[:, :], decay1[:, :], None, ALU.mult))
            vec.wait_ge(q_act, A_XR0)
            vec.wait_ge(d_ln, 16 * (2 + NB * (2 + NQ)))
            prep(V.reduce_sum(stat[:, 0:1], crow[:, :], axis=AX.X))
            prep(V.tensor_scalar(stat[:, 1:2], stat[:, 0:1], -1.0 / D, None, ALU.mult))
            prep(V.tensor_scalar(lnc[:, :], crow[:, :], stat[:, 1:2], None, ALU.add))
            prep(V.tensor_tensor(lnq[:, :], lnc[:, :], lnc[:, :], ALU.mult))
            prep(V.reduce_sum(stat[:, 4:5], lnq[:, :], axis=AX.X))
            prep(V.tensor_scalar(stat[:, 2:3], stat[:, 4:5], 1.0 / D, LN_EPS, ALU.mult, ALU.add))
            assert n[0] == V_LNVAR, n[0]
            vec.wait_ge(q_act, A_SQRT)
            prep(V.reciprocal(stat[:, 5:6], stat[:, 3:4]))
            prep(V.tensor_scalar(lnc[:, :], lnc[:, :], stat[:, 5:6], None, ALU.mult))
            prep(V.tensor_tensor(lnc[:, :], lnc[:, :], lng[:, :], ALU.mult))
            prep(V.tensor_tensor(ae, lnc[:, :], lnb[:, :], ALU.add))
            assert n[0] == V_AE, n[0]
            vec.wait_ge(q_pe, PE_AET)
            prep(V.tensor_copy(aeT[:, :, :], psS[:, 0:KB * NB].rearrange("p (k n) -> p k n", n=NB)))
            assert n[0] == V_AET, n[0]
            for q in range(W2R):
                vec.wait_ge(q_pe, PE_W2 + q + 1)
                for c in range(NQ):
                    src = (psA, psB)[q % 2][QC * c:QC * c + NB, 0:W2C // NQ].rearrange("p (d r) -> p r d", r=RANK)
                    add = b2s[QC * c:QC * c + NB, q, :].rearrange("p (d r) -> p r d", r=RANK)
                    prep(V.tensor_tensor(xw[QC * c:QC * c + NB, q, :, :], src, add, ALU.add), wait=False)
            vec.wait_ge(q_vec, n[0])
            assert n[0] == V_XW, n[0]
            vec.wait_ge(q_id, 2)
            for b in range(KB):
                d = baseI[:, b, P * b:P * (b + 1)]
                prep(V.scalar_tensor_tensor(out=d, in0=ident[:, :], scalar=2.0, in1=d, op0=ALU.mult, op1=ALU.add))
            for u in range(NB * KB):
                vec.wait_ge(q_pe, PE_LAYER + u + 1)
                prep(V.tensor_tensor(layer[:, u // KB, u % KB, :], (psA, psB)[u % 2][:, :], baseI[:, u % KB, :], ALU.add))
                assert n[0] == V_LAYER + u + 1, n[0]
            prep(V.tensor_tensor(xr_cur[:, :, 0, :], xr_cur[:, :, 0, :], h0r[:, :, :], ALU.add))
            meet(vec, "vec")

            def body(_i, known, w):
                n = [0]

                def link(ins):
                    n[0] += 1
                    ins.then_inc(S["vec_done"], 1)
                    vec.wait_ge(S["vec_done"], n[0])

                def mark(ins):
                    n[0] += 1
                    ins.then_inc(S["vec_done"], 1)
                    return n[0]

                if known == 2:
                    link(V.tensor_tensor(xl_cur[:, 0, :, :], xl_cur[:, 0, :, :], h0l[:, :, :], ALU.add))
                for s in range(CT):
                    if w["lstm"]:
                        vec.wait_ge(S["lstm_mm"], s + 1)
                        link(V.transpose(tr[:, :, :].rearrange("p g r -> p (g r)"), psL[:, :]))
                        link(V.scalar_tensor_tensor(out=l_s1[:, :, :], in0=tr[:, :, 0:NB], scalar=unscale[:, 1:2],
                                                    in1=xl_cur[:, s, :, :], op0=ALU.mult, op1=ALU.add))
                        V.scalar_tensor_tensor(out=l_s2[:, :, :], in0=tr[:, :, NB:2 * NB], scalar=unscale[:, 1:2],
                                               in1=l_s1[:, :, :], op0=ALU.mult, op1=ALU.add).then_inc(S["lstm_summed"], 1)
                    if w["rnn"]:
                        vec.wait_ge(S["rnn_mm"], s + 1)
                        link(V.scalar_tensor_tensor(out=r_s1[:, :, :], in0=ps_rnn[:, :, 0, :], scalar=unscale[:, 0:1],
                                                    in1=xr_cur[:, :, s, :], op0=ALU.mult, op1=ALU.add))
                        V.scalar_tensor_tensor(out=r_s2[:, :, :], in0=ps_rnn[:, :, 1, :], scalar=unscale[:, 0:1],
                                               in1=r_s1[:, :, :], op0=ALU.mult, op1=ALU.add).then_inc(S["rnn_summed"], 1)
                    if w["lstm"]:
                        vec.wait_ge(S["lstm_gated"], s + 1)
                        V.scalar_tensor_tensor(out=c_f[:, :], in0=gate[:, 1, :], scalar=1.0, in1=cell[:, :],
                                               op0=ALU.add, op1=ALU.mult).then_inc(S["vec_done"], 1)
                        n[0] += 1
                        link(V.scalar_tensor_tensor(out=c_i[:, :], in0=gate[:, 0, :], scalar=1.0, in1=gate[:, 3, :],
                                                    op0=ALU.add, op1=ALU.mult))
                        V.scalar_tensor_tensor(out=cell[:, :], in0=c_f[:, :], scalar=0.5, in1=c_i[:, :],
                                               op0=ALU.mult, op1=ALU.add).then_inc(S["lstm_cell"], 1)
                        o_at = mark(V.tensor_scalar(o_s[:, :], gate[:, 2, :], 1.0, H_SCALE, ALU.add, ALU.mult))
                    if w["rnn"]:
                        vec.wait_ge(S["rnn_tanh"], s + 1)
                        link(V.tensor_scalar(hrs[:, :, 0, :], hr[:, :, s, :], R_SCALE, None, ALU.mult))
                        V.scalar_tensor_tensor(out=hrs[:, :, 1, :], in0=hr[:, :, s, :], scalar=R_SCALE, in1=hrs[:, :, 0, :],
                                               op0=ALU.mult, op1=ALU.subtract).then_inc(S["rnn_h_ready"], 1)
                    if w["lstm"]:
                        vec.wait_ge(S["lstm_tanhc"], s + 1)
                        if not w["rnn"]:
                            vec.wait_ge(S["vec_done"], o_at)
                        o3 = o_s[:, :].rearrange("p (b n) -> p b n", b=KB)
                        t3 = tc[:, :].rearrange("p (b n) -> p b n", b=KB)
                        mark(V.tensor_tensor(hls[:, :, 0, :], o3, t3, ALU.mult))
                        link(V.tensor_tensor(hl[:, :, s, :], o3, t3, ALU.mult))
                        V.tensor_tensor(hls[:, :, 1, :], hl[:, :, s, :], hls[:, :, 0, :], ALU.subtract).then_inc(S["lstm_h_ready"], 1)

                    if w["mid"]:
                        if s < KB:
                            for k in range(TAPS):
                                xs = x1T[:, s, k:k + CT, :]
                                if k == 0:
                                    link(V.tensor_scalar(conv[:, s, :, :], xs, condT[:, s, 0:1], b_conv[:, s:s + 1], ALU.mult, ALU.add))
                                elif k < TAPS - 1:
                                    link(V.scalar_tensor_tensor(out=conv[:, s, :, :], in0=xs, scalar=condT[:, s, k:k + 1],
                                                                in1=conv[:, s, :, :], op0=ALU.mult, op1=ALU.add))
                                else:
                                    V.scalar_tensor_tensor(out=conv[:, s, :, :], in0=xs, scalar=condT[:, s, k:k + 1],
                                                           in1=conv[:, s, :, :], op0=ALU.mult, op1=ALU.add).then_inc(S["conv_ready"], 1)
                        if s == SOFT_STEP + 1:
                            vec.wait_ge(S["c_ready"], 1)
                            mark(V.tensor_scalar(zmax[:, :], psS[0:NS, 0:TOK], b_B[:, :], 0.0, ALU.add, ALU.max))
                            link(V.tensor_scalar(drive[:, :], psS[0:NS, 2 * TOK:3 * TOK], b_u[:, :], spt[:, 1:2], ALU.add, ALU.mult))
                        if SOFT_STEP < s <= SOFT_STEP + 3:
                            if s == SOFT_STEP + 1:
                                vec.wait_ge(S["exp_ready"], 1)
                            softplus(V, link, zmax[:, :], ez[:, :], den[:, :], rden[:, :], sr[:, :], qr[:, :],
                                     pol[:, 0, :], pol[:, 1, :], bt[:, :], third=s - SOFT_STEP - 1)
                        if s == SOFT_STEP + 4:
                            link(V.tensor_tensor(drive[:, :], drive[:, :], bt[:, :], ALU.mult))
                            dv = drive[:, :].rearrange("p (t n) -> p t n", n=NB)
                            for b in range(NB):
                                mark(V.tensor_tensor_scan(states[:, :, b], decay[:, :], dv[:, :, b], st0[:, b:b + 1], ALU.mult, ALU.add))
                            vec.wait_ge(S["vec_done"], n[0])
                            mark(V.tensor_copy(st0[:, :], states[:, CT - 1, :]))
                            V.tensor_tensor(y[:, :], states[:, :, :].rearrange("p t n -> p (t n)"), ct[:, :], ALU.mult).then_inc(S["y_ready"], 1)
                        if s == WO_STEP + 1:
                            vec.wait_ge(S["wo_mm"], 1)
                            for b in range(KB):
                                V.scalar_tensor_tensor(out=x2_nxt[:, b, :, :], in0=psX[:, TOK * b:TOK * (b + 1)].rearrange("p (t n) -> p t n", n=NB),
                                                       scalar=b_out[:, b:b + 1], in1=x1T[:, b, HALO:HALO + CT, :],
                                                       op0=ALU.add, op1=ALU.add).then_inc(S["x2_ready"], 1)
                    if w["out"] and s == 5:
                        vec.wait_ge(S["out_mm"], 1)
                        V.tensor_copy(orow[:, :], psOut[:, :]).then_inc(S["out_ready"], 1)
                meet(vec, "vec")

            pipeline(vec, body)

        @block.tensor
        def _(pe):
            mm = nc.tensor.matmul
            pe.wait_ge(d_rnnw, 16 * (3 + NB))
            for m in range(KB):
                for k in range(KB):
                    w_ = whr32[:, k, P * m:P * (m + 1)]
                    mm(psR[:, NB * m:NB * (m + 1)], w_, condT[:, k, :], start=(k == 0), stop=(k == KB - 1))
            pe.wait_ge(q_id, 2)
            pe.wait_ge(d_x0, 16)
            for b in range(KB):
                last = x_transpose(mm, xrow, psX, ident, b)
            last.then_inc(q_pe, 1)
            pe.wait_ge(q_act, A_XT0)
            for m in range(KB):
                for k in range(KB):
                    last = rnn_in(mm, wxr, xT_cur, psI, m, k)
                last.then_inc(q_pe, 1)
            pe.wait_ge(d_lstmw, 16)
            for g in range(G):
                for m in range(KB):
                    for k in range(KB):
                        w_ = whl32[:, k, g * D + P * m:g * D + P * (m + 1)]
                        o = 64 + (g * KB + m) * NB
                        last = mm(psR[:, o:o + NB], w_, condT[:, k, :], start=(k == 0), stop=(k == KB - 1))
            last.then_inc(q_pe, 1)
            pe.wait_ge(q_vec, V_AE)
            for k in range(KB):
                last = mm(psS[:, NB * k:NB * (k + 1)], ae[:, P * k:P * (k + 1)], ident[0:NB, 0:NB], start=True, stop=True)
            last.then_inc(q_pe, 1)
            pe.wait_ge(q_vec, V_AET)
            pe.wait_ge(d_w1, 16)
            for m in range(KB):
                for k in range(KB):
                    last = mm(psB[:, NB * m:NB * (m + 1)], w1s[:, k, P * m:P * (m + 1)], aeT[:, k, :], start=(k == 0), stop=(k == KB - 1))
                last.then_inc(q_pe, 1)
            pe.wait_ge(q_act, A_GELU)
            for q in range(W2R):
                pe.wait_ge(d_w2[q % 2], 16 * (q // 2 + 1))
                if q >= 2:
                    pe.wait_ge(q_vec, V_AET + NQ * (q - 1))
                wd = W2C // NQ
                for k in range(KB):
                    for c in range(NQ):
                        last = mm((psA, psB)[q % 2][QC * c:QC * c + NB, 0:wd], hmT[:, k, :], w2s[q % 2][:, k, wd * c:wd * (c + 1)],
                                  start=(k == 0), stop=(k == KB - 1), tile_position=(0, QC * c))
                last.then_inc(q_pe, 1)
            pe.wait_ge(d_xab, 16 * 2 * NQ * NB * (W2R // 2))
            pe.wait_ge(q_vec, V_XW)
            for u in range(NB * KB):
                if u >= 2:
                    pe.wait_ge(q_vec, V_LAYER + u - 1)
                w_ = xab[:, u // KB, P * (u % KB):P * (u % KB + 1)]
                mm((psA, psB)[u % 2][:, :], w_, xbb[:, u // KB, :], start=True, stop=True).then_inc(q_pe, 1)
            meet(pe, "pe")

            def body(_i, _known, w):
                for s in range(CT):
                    if w["lstm"]:
                        if s > 0:
                            pe.wait_ge(S["lstm_h_ready"], s)
                        for k in range(KB):
                            for e in range(2):
                                for j in range(NQ):
                                    last = mm(psL[QC * j:QC * j + 2 * NB, :], hls[:, k, :, :].rearrange("p s n -> p (s n)"),
                                              whl[:, k, e, j, :], start=(k == 0 and e == 0), stop=(k == KB - 1 and e == 1),
                                              tile_position=(0, QC * j))
                        last.then_inc(S["lstm_mm"], 1)
                    if w["rnn"]:
                        if s > 0:
                            pe.wait_ge(S["rnn_h_ready"], s)
                        for m in range(KB):
                            for k in range(KB):
                                for e in range(2):
                                    last = mm(psR[:, m * 2 * NB:(m + 1) * 2 * NB], whr[:, k, e, m, :],
                                              hrs[:, k, :, :].rearrange("p s n -> p (s n)"),
                                              start=(k == 0 and e == 0), stop=(k == KB - 1 and e == 1))
                        last.then_inc(S["rnn_mm"], 1)

                    if w["out"] and s < KB:
                        for n in range(NB):
                            last = mm(psOut[CT * n:CT * (n + 1), :], x3T[:, s, :, n], layer[:, n, s, :],
                                      start=(s == 0), stop=(s == KB - 1), tile_position=(0, CT * n))
                        if s == KB - 1:
                            last.then_inc(S["out_mm"], 1)
                    if w["l0"] and s == XT_STEP:
                        pe.wait_ge(S["x_arrived"], 16)
                        for b in range(KB):
                            last = x_transpose(mm, xrow, psX, ident, b)
                        last.then_inc(S["xT_mm"], 1)
                    if w["mid"] and SSM_STEP <= s < SSM_STEP + 3:
                        c = s - SSM_STEP
                        if c == 0:
                            pe.wait_ge(S["conv_ready"], KB)
                        for k in range(KB):
                            w_ = wp[:, k, NS * c:NS * (c + 1)] if c < 2 else ws[:, k, :]
                            r_ = conv[:, k, :, :] if c < 2 else x1T[:, k, HALO:HALO + CT, :]
                            last = mm(psS[0:NS, TOK * c:TOK * (c + 1)], w_, r_.rearrange("p t n -> p (t n)"),
                                      start=(k == 0), stop=(k == KB - 1))
                        if c == 2:
                            last.then_inc(S["ssm_mm"], 1)
                    if w["l0"] and L0_STEP <= s < L0_STEP + KB:
                        if s == L0_STEP:
                            pe.wait_ge(S["xT_ready"], 1)
                        for k in range(KB):
                            last = rnn_in(mm, wxr, xT_nxt, psI, s - L0_STEP, k)
                        last.then_inc(S["l0_mm"], 1)
                    if w["mid"] and s == WO_STEP:
                        pe.wait_ge(S["y_ready"], 1)
                        for b in range(KB):
                            w_ = wo[:, P * b:P * (b + 1)]
                            last = mm(psX[:, TOK * b:TOK * (b + 1)], w_, y[:, :], start=True, stop=True)
                        last.then_inc(S["wo_mm"], 1)
                    if w["mid"] and s >= L2_STEP:
                        for u in range(L2_MM * (s - L2_STEP), min(L2_MM * (s - L2_STEP + 1), L2_ALL)):
                            g, b, k = u // (KB * KB), u // KB % KB, u % KB
                            if u == 0:
                                pe.wait_ge(S["x2_ready"], KB)
                            if g >= 2 and b == 0 and k == 0:
                                pe.wait_ge(S["l2_ready"], KB * (g - 1))
                            w_ = wxl[:, k, g * D + P * b:g * D + P * (b + 1)]
                            last = mm((psA, psB)[g % 2][:, TOK * b:TOK * (b + 1)], w_, x2_nxt[:, k, :, :].rearrange("p t n -> p (t n)"),
                                      start=(k == 0), stop=(k == KB - 1))
                            if b == KB - 1 and k == KB - 1:
                                last.then_inc(S["l2_mm"], 1)
                meet(pe, "pe")

            pipeline(pe, body)


def x_transpose(mm, xrow, psX, ident, b):
    w_ = xrow[:, P * b:P * (b + 1)]
    return mm(psX[:, TOK * b:TOK * (b + 1)], w_, ident[:, :], start=True, stop=True)


def rnn_in(mm, wxr, xT, psI, m, k):
    w_ = wxr[:, k, P * m:P * (m + 1)]
    return mm(psI[:, TOK * m:TOK * (m + 1)], w_, xT[:, k, :, :].rearrange("p t n -> p (t n)"),
              start=(k == 0), stop=(k == KB - 1))


def softplus(V, link, zmax, ez, den, rden, s, q, pa, pb_, out, third=None):
    if third in (None, 0):
        link(V.tensor_scalar(den, ez, 2.0, None, ALU.add))
        link(V.reciprocal(rden, den))
        link(V.tensor_tensor(s, ez, rden, ALU.mult))
        link(V.tensor_tensor(q, s, s, ALU.mult))
        link(V.tensor_scalar(pa, q, 1.0 / 15, None, ALU.mult))
    if third in (None, 1):
        link(V.scalar_tensor_tensor(out=pb_, in0=pa, scalar=1.0 / 13, in1=q, op0=ALU.add, op1=ALU.mult))
        link(V.scalar_tensor_tensor(out=pa, in0=pb_, scalar=1.0 / 11, in1=q, op0=ALU.add, op1=ALU.mult))
        link(V.scalar_tensor_tensor(out=pb_, in0=pa, scalar=1.0 / 9, in1=q, op0=ALU.add, op1=ALU.mult))
        link(V.scalar_tensor_tensor(out=pa, in0=pb_, scalar=1.0 / 7, in1=q, op0=ALU.add, op1=ALU.mult))
    if third in (None, 2):
        link(V.scalar_tensor_tensor(out=pb_, in0=pa, scalar=1.0 / 5, in1=q, op0=ALU.add, op1=ALU.mult))
        link(V.scalar_tensor_tensor(out=pa, in0=pb_, scalar=1.0 / 3, in1=q, op0=ALU.add, op1=ALU.mult))
        link(V.scalar_tensor_tensor(out=pb_, in0=pa, scalar=1.0, in1=s, op0=ALU.add, op1=ALU.mult))
        link(V.scalar_tensor_tensor(out=out, in0=pb_, scalar=2.0, in1=zmax, op0=ALU.mult, op1=ALU.add))


V_RSPLIT = 1 + 5 + 2 * KB * KB
V_LMAX = V_RSPLIT + 6 + 1
V_SPLIT = V_LMAX + 5 + 3 * KB * G
V_DECAY = V_SPLIT + 1 + G + 2 + 13 + 4
V_LNVAR = V_DECAY + 6
V_AE = V_LNVAR + 4
V_AET = V_AE + 1
V_XW = V_AET + W2R * NQ
V_LAYER = V_XW + KB
PE_X0 = 1
PE_H0 = PE_X0 + KB + 1
PE_AET = PE_H0 + 1
PE_W1 = PE_AET
PE_W2 = PE_W1 + KB
PE_LAYER = PE_W2 + W2R
A_XT0 = 1
A_XR0 = A_XT0 + KB
A_EXP0 = A_XR0 + 2
A_SQRT = A_EXP0 + 1
A_GELU = A_SQRT + KB

_INS = ['x', 'cond_1024', 'L0_cond_Wx', 'L0_cond_Wh', 'L0_cond_b', 'L1_cond_conv_b', 'L1_cond_Wp', 'L1_cond_bp',
        'L1_cond_Ws', 'L1_cond_bs', 'L1_cond_A_log', 'L1_cond_dt_log', 'L1_cond_Wo', 'L1_cond_bo', 'L2_cond_Wx',
        'L2_cond_Wh', 'L2_cond_b', 'L3_cond_base_layer', 'L3_cond_w1', 'L3_cond_b1', 'L3_cond_w2', 'L3_cond_b2',
        'L3_cond_ln_g', 'L3_cond_ln_b']


def kernel(**inputs):
    import concourse.bacc as bacc
    from concourse.bass_utils import run_bass_kernel_spmd

    nc = bacc.Bacc("TRN2", target_bir_lowering=False, num_devices=1)
    arrays, args = {}, []
    for name in _INS:
        a = np.ascontiguousarray(inputs[name])
        arrays[f"in_{name}"] = a
        args.append(nc.dram_tensor(f"in_{name}", a.shape, mybir.dt.from_np(a.dtype), kind="ExternalInput").ap())
    out = nc.dram_tensor("out_0", (NB, T, D), F32, kind="ExternalOutput").ap()
    resid_stack_kernel(nc, *args, out)
    r = run_bass_kernel_spmd(nc, [arrays], core_ids=[0])
    return r.results[0]["out_0"]
```

```python
import numpy as np
import concourse.bass as bass
from concourse import mybir
from contextlib import ExitStack

F32 = mybir.dt.float32
F16 = mybir.dt.float16
U32 = mybir.dt.uint32
ALU = mybir.AluOpType
ACT = mybir.ActivationFunctionType
AX = mybir.AxisListType
RMAX = bass.bass_isa.ReduceOp.max

P = 128
NB, T, D = 4, 1024, 512
CT = 32
NCH = T // CT
TOK = NB * CT
KB = D // P
QC = 32
NQ = P // QC
G = 4
GB = G * KB
NS = 64
TAPS = 4
RANK = 8
LN_EPS = 1e-5
H_SCALE = 4096.0
R_SCALE = 8192.0
NH = 2
HB = KB // NH
HG = G * HB
HW = HG * QC
LO = 16
XS = 2 * LO
PIECES = [(0, 12), (12, 24), (24, 30), (30, 32)]
W2C = 1024
W2R = 2 * D * RANK // W2C
DP = W2C // NQ // RANK

XT_STEP = 0
OUT_STEPS = [1, 2, 3, 11]
SSM_STEP = 4
L0_STEP = 7
SCAN_STEP = 11
WO_STEP = 12
L2_STEP = 14
L2_MM = 4
L2_ALL = GB * KB


def l2_last_step(g):
    return L2_STEP + (KB * KB * (g + 1) - 1) // L2_MM


def chunk_work(i):
    return dict(rnn=0 <= i < NCH, l0=i + 1 < NCH, l0_after=i + 2 < NCH, mid=1 <= i <= NCH, lstm=2 <= i <= NCH + 1, out=3 <= i <= NCH + 2)


FIRST_FULL, LAST_FULL = 3, NCH - 4
assert (LAST_FULL + 1 - FIRST_FULL) % 2 == 0
HEAD = list(range(0, FIRST_FULL))
TAIL = list(range(LAST_FULL + 1, NCH + 3))


def resid_stack_kernel(nc, x, cond, l0_Wx, l0_Wh, l0_b, conv_b, Wp, bp, Ws, bs, A_log, dt_log, Wo, bo,
                       l2_Wx, l2_Wh, l2_b, base, w1, b1, w2, b2, ln_g, ln_b, out):
    ctx = ExitStack()
    with ctx:
        def sb(name, shape, dt=F32):
            return ctx.enter_context(nc.sbuf_tensor(name, shape, dt))

        def pb(name):
            return ctx.enter_context(nc.psum_tensor(name, [P, 512], F32))

        def sem(name):
            return ctx.enter_context(nc.semaphore(name))

        stage = sb("stage", [P, 5 * 2048])

        def reuse(at):
            return stage[:, at * KB * TOK:(at + 1) * KB * TOK]

        whl = sb("lstm_Wh_parts", [P, KB, NH, 2, NQ, HW], F16)
        whr = sb("rnn_Wh_parts", [P, KB, 2, KB, P], F16)
        wxl = sb("lstm_Wx", [P, KB, G * D])
        wxr = sb("rnn_Wx", [P, KB, D])
        wp = sb("ssm_Wp", [P, KB, 2 * NS])
        ws = sb("ssm_Ws", [P, KB, NS])
        wo = sb("ssm_Wo", [NS, D])
        layer = sb("layer_plus_2I", [P, NB, KB, D])
        condT = sb("condT", [P, KB, NB])
        b_rnn = sb("b_rnn", [P, KB])
        b_lstm = sb("b_lstm", [P, GB])
        b_lsc = sb("b_lstm_scaled", [P, NH, G, HB])
        b_conv = sb("b_conv", [P, KB])
        b_out = sb("b_ssm_out", [P, KB])
        b_B = sb("b_B", [NS, 1])
        b_C = sb("b_C", [NS, 1])
        b_u = sb("b_u", [NS, 1])
        ab = sb("A_dt_log", [NS, 2])
        spt = sb("softplus_A_dt", [NS, 2])
        decay = sb("decay", [NS, CT])
        decay1 = sb("decay1", [NS, 1])
        ident = sb("ident", [P, P])
        wmax = sb("wmax", [P, 2])
        wmaxa = sb("wmaxa", [P, 2])
        wpow = sb("wpow", [P, 2])
        wscale = sb("wscale", [P, 2])
        unscale = sb("unscale", [P, 2])
        xscale = sb("lstm_in_scale", [P, 2])
        h0r = sb("h0_rnn", [P, KB, NB])
        h0l = sb("h0_lstm", [P, NH, G, HB, NB])
        def hidden(v):
            return v.rearrange("p (b t n) -> p b t n", b=KB, t=CT)

        HALO = TAPS - 1
        xrow = sb("x_rows", [P, D])
        xT = [sb("xT_0", [P, KB, CT, NB])[:, :, :, :], hidden(reuse(0))]
        xr = [sb("rnn_in_0", [P, KB, CT, NB])[:, :, :, :], hidden(reuse(1))]
        hr = sb("rnn_h", [P, KB, CT, NB])
        x1T = [sb(f"x1T_{e}", [P, KB, HALO + CT, NB]) for e in range(2)]
        x2 = sb("x2", [P, KB, CT, NB])
        x2s = [sb("x2_scaled_0", [P, KB, CT, NB])[:, :, :, :], hidden(reuse(2))]
        xl = [sb(f"lstm_in_{e}", [P, CT, GB, NB]) for e in range(2)]
        hl = sb("lstm_h_scaled", [P, KB, CT, NB])
        x3s = [sb("x3_scaled_0", [P, KB, CT, NB])[:, :, :, :], hidden(reuse(8))]
        orow = sb("out_rows", [P, D])
        hrs = sb("rnn_h_parts", [P, KB, 2, NB], F16)
        hls = sb("lstm_h_parts", [P, KB, LO + NB], F16)
        r_s1 = sb("rnn_sum1", [P, KB, NB])
        r_s2 = sb("rnn_sum2", [P, KB, NB])
        tr = [[sb(f"lstm_sums_{h}{e}", [P, HG, XS + NB]) for e in range(2)] for h in range(NH)]
        arg = [sb(f"lstm_arg{h}", [P, HG, NB]) for h in range(NH)]
        gate = [sb(f"lstm_gates{h}", [P, G, HB * NB]) for h in range(NH)]
        cell = [sb(f"lstm_2c{h}", [P, HB * NB]) for h in range(NH)]
        c_f = [sb(f"lstm_f_part{h}", [P, HB * NB]) for h in range(NH)]
        c_i = [sb(f"lstm_i_part{h}", [P, HB * NB]) for h in range(NH)]
        o_s = [sb(f"lstm_o_scaled{h}", [P, HB * NB]) for h in range(NH)]
        tc = [sb(f"lstm_tanh_c{h}", [P, HB * NB]) for h in range(NH)]
        conv = hidden(reuse(3))
        taps = [hidden(reuse(9 + k)) for k in range(TAPS - 1)]
        zabs, zmax, ez, uu, den, rden, sr, qr, bt, ct, drive, y, pol_a, pol_b, st_ = [
            stage[:, 4 * 512 + TOK * q:4 * 512 + TOK * (q + 1)] for q in range(15)]
        zabs, zmax, ez, uu, den, rden, sr, qr, bt, ct, drive, y, pol_a, pol_b, st_ = [
            v[0:NS, :] for v in (zabs, zmax, ez, uu, den, rden, sr, qr, bt, ct, drive, y, pol_a, pol_b, st_)]
        states = st_.rearrange("p (t n) -> p t n", n=NB)
        st0 = sb("state0", [NS, NB])
        spw = sb("softplus_work", [NS, 8, 2])
        whl32 = stage[:, 0:8192].rearrange("p (k n) -> p k n", k=KB)
        whr32 = stage[:, 8192:10240].rearrange("p (k n) -> p k n", k=KB)
        w1s = whr32
        w2s = [stage[:, h * 4096:(h + 1) * 4096].rearrange("p (k n) -> p k n", k=KB) for h in range(2)]
        b2s = xl[1][:, :, :, :].rearrange("p t g n -> p (t g n)").rearrange("p (q n) -> p q n", q=W2R)
        xw = xl[0][:, :, :, :].rearrange("p t g n -> p (t g n)").rearrange("p (q r d) -> p q r d", q=W2R, r=RANK)
        xab = stage[0:RANK, 8192:10240].rearrange("p (n d) -> p n d", n=NB)
        xbb = stage[0:RANK, 0:2048].rearrange("p (n d) -> p n d", n=NB)
        baseI = layer[:, NB - 1, :, :]
        ae = orow[0:NB, :]
        crow, lng, lnb, lnc, lnq = [t[0:NB, :, :, :].rearrange("p b t n -> p (b t n)") for t in (x2, x2s[0], x3s[0], hl, hr)]
        stat = sb("ln_stat", [NB, 8])
        aeT = sb("aeT", [P, KB, NB])
        hmT = sb("hmT", [P, KB, NB])
        b1T = sb("b1T", [P, KB])

        psL0, psL1, psR, psOut, psX, psS, psA, psB = [pb(n) for n in
            ("ps_lstm0", "ps_lstm1", "ps_rnn", "ps_out", "ps_x", "ps_ssm", "ps_lstm_in_a", "ps_lstm_in_b")]
        psL = (psL0, psL1)
        psI = psA
        ps_rnn = psR[:, 0:KB * 2 * NB].rearrange("p (m s n) -> p m s n", m=KB, s=2)

        d_rnnw, d_x0, d_lstmw, d_small, d_w1, d_w2a, d_w2b, d_xab, d_ln = [sem(n) for n in
            ("d_rnnw", "d_x0", "d_lstmw", "d_small", "d_w1", "d_w2a", "d_w2b", "d_xab", "d_ln")]
        d_w2 = [d_w2a, d_w2b]
        q_id, q_zero, q_vec, q_pool, q_pe, q_act = [sem(n) for n in
            ("q_id", "q_zero", "q_vec", "q_pool", "q_pe", "q_act")]
        arrive = sem("engines_arrived")
        x_arrived = sem("x_arrived")
        go = {e: sem(f"go_{e}") for e in ("pe", "act", "vec", "pool")}
        names = [f"{n}{h}" for h in range(NH) for n in ("lstm_mm", "lstm_summed", "lstm_gated", "lstm_cell", "lstm_tanhc",
                                                        "lstm_h_ready", "lstm_in_ready")]
        names += ["rnn_mm", "rnn_summed", "rnn_tanh", "rnn_h_ready", "vec_done", "pool_done", "act_done",
                  "tap_ready", "xT_mm", "xT_ready", "l0_mm", "l0_ready", "conv_ready", "ssm_mm", "ssm_out", "exp_ready", "recip_ready",
                  "den_ready", "drive_ready", "scan_ready", "y_ready", "wo_mm", "wo_out", "x2_scaled",
                  "x2_ready", "l2_mm", "l2_ready", "out_mm", "out_ready", "out_stored"]
        S = {n: sem(n) for n in names}
        nums = sorted(s.num for s in S.values())
        assert nums == list(range(nums[0], nums[0] + len(nums)))
        chunk_sems = range(nums[0], nums[-1] + 1)

        block = ctx.enter_context(nc.Block())

        def rows(w):
            return w.rearrange("(k p) n -> p k n", p=P)

        def column(v):
            return v.rearrange("(k p) -> p k", p=P)

        def pipeline(eng, body):
            for i in HEAD:
                body(i, i % 2, i, chunk_work(i))
            with eng.Fori(FIRST_FULL, LAST_FULL + 1, 2) as i:
                for h in range(2):
                    body(i + h, (FIRST_FULL + h) % 2, None, chunk_work(FIRST_FULL + h))
            for i in TAIL:
                body(i, i % 2, i, chunk_work(i))

        def meet(eng, name):
            eng.drain().then_inc(arrive, 1)
            eng.wait_ge(go[name], 1)
            eng.sem_clear(go[name])

        @block.sync
        def _(sp):
            x_v = x.rearrange("n (i t) d -> i n t d", t=CT)
            out_v = out.rearrange("n (i t) d -> i n t d", t=CT)
            with nc.allow_non_contiguous_dma("weights in hidden layout"):
                sp.dma_start(whr32, rows(l0_Wh)).then_inc(d_rnnw, 16)
                sp.dma_start(wxr[:, :, :], rows(l0_Wx)).then_inc(d_rnnw, 16)
                for n in range(NB):
                    sp.dma_start(condT[:, :, n], column(cond[n])).then_inc(d_rnnw, 16)
                sp.dma_start(b_rnn[:, :], column(l0_b)).then_inc(d_rnnw, 16)
                sp.dma_start(xrow[:, :], x_v[0]).then_inc(d_x0, 16)
                sp.dma_start(whl32, rows(l2_Wh)).then_inc(d_lstmw, 16)
                cut = lambda v, a: v[a:a + NS].rearrange("(p o) -> p o", o=1)
                for dst, src in ((b_lstm[:, :], column(l2_b)), (b_conv[:, :], column(conv_b)), (b_out[:, :], column(bo)),
                                 (b_B[:, :], cut(bp, 0)), (b_C[:, :], cut(bp, NS)), (b_u[:, :], cut(bs, 0)),
                                 (ab[:, 0:1], cut(A_log, 0)), (ab[:, 1:2], cut(dt_log, 0)),
                                 (wp[:, :, :], rows(Wp)), (ws[:, :, :], rows(Ws)), (wo[:, :], Wo[:, :]),
                                 (wxl[:, :, :], rows(l2_Wx)), (baseI, rows(base))):
                    sp.dma_start(dst, src).then_inc(d_small, 16)
                row = lambda v: v.rearrange("(o n) -> o n", o=1)
                sp.dma_start(crow[:, :], cond[:, :]).then_inc(d_ln, 16)
                for n in range(NB):
                    sp.dma_start(lng[n:n + 1, :], row(ln_g)).then_inc(d_ln, 16)
                    sp.dma_start(lnb[n:n + 1, :], row(ln_b)).then_inc(d_ln, 16)
                    for q in range(NQ):
                        src = b2.rearrange("(a q g d) -> a q g d", a=1, g=NQ, d=W2C // NQ)[:, :, q, :]
                        sp.dma_start(b2s[QC * q + n:QC * q + n + 1, :, :], src).then_inc(d_ln, 16)
                sp.dma_start(b1T[:, :], column(b1)).then_inc(d_ln, 16)
                sp.wait_ge(q_vec, V_SPLIT)
                sp.wait_ge(q_pe, PE_H0)
                sp.dma_start(w1s, rows(w1)).then_inc(d_w1, 16)
                w2v = w2.rearrange("(k p) (q n) -> q p k n", p=P, n=W2C)
                for q in range(W2R):
                    if q >= 2:
                        sp.wait_ge(q_pe, PE_W2 + q - 1)
                    sp.dma_start(w2s[q % 2], w2v[q]).then_inc(d_w2[q % 2], 16)
                sp.wait_ge(q_vec, V_XW)
                for half, dst in ((0, xab), (1, xbb)):
                    for q in range(NQ):
                        for n in range(NB):
                            for a in range(W2R // 2):
                                f = P * a + DP * q
                                sp.dma_start(dst[:, n, f:f + DP], xw[QC * q + n:QC * q + n + 1, half * (W2R // 2) + a, :, :]
                                             ).then_inc(d_xab, 16)

            def body(i, _par, _known, w):
                if w["l0_after"]:
                    sp.wait_ge(S["xT_mm"], 1)
                    sp.dma_start(xrow[:, :], x_v[i + 2]).then_inc(x_arrived, 16)
                if w["out"]:
                    sp.wait_ge(S["out_ready"], 1)
                    for n in range(NB):
                        sp.dma_start(out_v[i - 3, n], orow[CT * n:CT * (n + 1), :]).then_inc(S["out_stored"], 16)
                    sp.wait_ge(S["out_stored"], 16 * NB)
                if w["l0_after"]:
                    sp.wait_ge(x_arrived, 16)
                    sp.sem_clear(x_arrived)
                sp.wait_ge(arrive, 4)
                sp.sem_clear(chunk_sems)
                sp.sem_clear(arrive)
                for e in go.values():
                    sp.sem_inc(e, 1)

            sp.wait_ge(q_pe, PE_X0)
            sp.dma_start(xrow[:, :], x_v[1]).then_inc(x_arrived, 16)
            sp.wait_ge(x_arrived, 16)
            sp.sem_clear(x_arrived)
            sp.wait_ge(arrive, 4)
            sp.sem_clear(arrive)
            for e in go.values():
                sp.sem_inc(e, 1)
            pipeline(sp, body)

        @block.gpsimd
        def _(pool):
            nc.gpsimd.memset(ident[:, :], 0.0).then_inc(q_id, 1)
            pool.wait_ge(q_id, 1)
            nc.gpsimd.affine_select(out=ident[:, :], in_=ident[:, :], compare_op=ALU.not_equal, fill=1.0, base=0,
                                    pattern=[[-1, P]], channel_multiplier=1).then_inc(q_id, 1)
            pool.wait_ge(q_vec, 1)
            nc.gpsimd.partition_all_reduce(wmaxa[:, 0:1], wmax[:, 0:1], P, RMAX).then_inc(q_pool, 1)
            pool.wait_ge(q_vec, V_LMAX)
            nc.gpsimd.partition_all_reduce(wmaxa[:, 1:2], wmax[:, 1:2], P, RMAX).then_inc(q_pool, 1)
            meet(pool, "pool")

            def body(_i, par, known, w):
                n = [0]

                def step(ins):
                    n[0] += 1
                    ins.then_inc(S["pool_done"], 1)
                    pool.wait_ge(S["pool_done"], n[0])

                Q = nc.gpsimd

                def fill(s):
                    for h in range(NH):
                        if s >= 2:
                            pool.wait_ge(S[f"lstm_summed{h}"], s - 1)
                        Q.tensor_copy(tr[h][s % 2][:, :, XS:XS + NB],
                                      xl[par][:, s, h * HG:(h + 1) * HG, :]).then_inc(S[f"lstm_in_ready{h}"], 1)

                def convolve(b):
                    pool.wait_ge(S["tap_ready"], TAPS * (b + 1))
                    for k in range(1, TAPS):
                        ins = Q.tensor_tensor(conv[:, b, :, :], conv[:, b, :, :], taps[k - 1][:, b, :, :], ALU.add)
                        if k < TAPS - 1:
                            step(ins)
                    ins.then_inc(S["conv_ready"], 1)

                def series(c, last=False):
                    step(Q.tensor_scalar(pol_b, pol_a, c, None, ALU.add))
                    step(Q.tensor_tensor(pol_a, pol_b, sr if last else qr, ALU.mult))

                def residuals(a, z):
                    ts = slice(a, z)
                    if w["rnn"]:
                        pool.wait_ge(S["rnn_tanh"], z)
                        step(Q.tensor_tensor(x1T[par][:, :, HALO + a:HALO + z, :], xT[par][:, :, ts, :], hr[:, :, ts, :], ALU.add))
                    if w["lstm"]:
                        for h in range(NH):
                            pool.wait_ge(S[f"lstm_h_ready{h}"], z)
                        step(Q.tensor_tensor(x3s[par][:, :, ts, :], x2s[par][:, :, ts, :], hl[:, :, ts, :], ALU.add))

                if known == 2:
                    step(Q.tensor_tensor(xl[par][:, 0, :, :], xl[par][:, 0, :, :],
                                         h0l[:, :, :, :, :].rearrange("p h g b n -> p (h g b) n"), ALU.add))
                if w["lstm"]:
                    fill(0)
                    fill(1)
                for s in range(CT):
                    if w["lstm"] and s + 2 < CT:
                        fill(s + 2)
                    if w["mid"]:
                        if 1 <= s <= KB:
                            convolve(s - 1)
                        if s == SSM_STEP + 3:
                            pool.wait_ge(S["exp_ready"], 1)
                            Q.tensor_scalar(den[:, :], ez[:, :], 2.0, None, ALU.add).then_inc(S["den_ready"], 1)
                            step(Q.tensor_scalar(drive[:, :], uu[:, :], spt[:, 1:2], None, ALU.mult))
                            pool.wait_ge(S["recip_ready"], 1)
                            step(Q.tensor_tensor(sr[:, :], ez[:, :], rden[:, :], ALU.mult))
                            step(Q.tensor_tensor(qr[:, :], sr[:, :], sr[:, :], ALU.mult))
                            step(Q.tensor_scalar(pol_a, qr[:, :], 1.0 / 15, None, ALU.mult))
                        if s == SSM_STEP + 4:
                            for c in (13, 11, 9, 7, 5):
                                series(1.0 / c)
                        if s == SSM_STEP + 5:
                            pool.wait_ge(S["ssm_out"], 3)
                            series(1.0 / 3)
                            series(1.0, last=True)
                            step(Q.tensor_scalar(pol_b, pol_a, 2.0, None, ALU.mult))
                            step(Q.tensor_tensor(bt[:, :], pol_b, zmax[:, :], ALU.add))
                            Q.tensor_tensor(drive[:, :], drive[:, :], bt[:, :], ALU.mult).then_inc(S["drive_ready"], 1)
                        if s == SCAN_STEP + 1:
                            pool.wait_ge(S["scan_ready"], 1)
                            Q.tensor_tensor(y[:, :], states[:, :, :].rearrange("p t n -> p (t n)"), ct[:, :], ALU.mult
                                            ).then_inc(S["y_ready"], 1)
                        if s == WO_STEP + 1:
                            pool.wait_ge(S["wo_out"], KB)
                            Q.tensor_tensor(x2[:, :, :, :], x2[:, :, :, :], x1T[1 - par][:, :, HALO:HALO + CT, :], ALU.add
                                            ).then_inc(S["x2_ready"], 1)
                    if w["rnn"] and w["mid"] and s == WO_STEP:
                        step(Q.tensor_copy(x1T[par][:, :, 0:HALO, :], x1T[1 - par][:, :, CT:CT + HALO, :]))
                    for a, z in PIECES:
                        if s == z:
                            residuals(a, z)
                if w["rnn"] or w["lstm"]:
                    residuals(*PIECES[-1])
                meet(pool, "pool")

            pipeline(pool, body)

        @block.scalar
        def _(act):
            act.wait_ge(q_pe, PE_X0)
            nc.scalar.activation(xT[0].rearrange("p b t n -> p b n t"),
                                 psX[:, :].rearrange("p (b n t) -> p b n t", b=KB, n=NB), ACT.Identity).then_inc(q_act, 1)
            act.wait_ge(q_pe, PE_X0 + KB)
            for m in range(KB):
                nc.scalar.activation(xr[0][:, m, :, :], psI[:, TOK * m:TOK * (m + 1)].rearrange("p (t n) -> p t n", n=NB),
                                     ACT.Identity, bias=b_rnn[:, m:m + 1]).then_inc(q_act, 1)
            act.wait_ge(d_small, 16 * 13)
            nc.scalar.activation(spw[:, 0, :], ab[:, :], ACT.Abs).then_inc(q_act, 1)
            act.wait_ge(q_act, A_XR0 + 1)
            nc.scalar.activation(spw[:, 1, :], spw[:, 0, :], ACT.Exp, scale=-1.0).then_inc(q_act, 1)
            act.wait_ge(q_vec, V_LNVAR)
            nc.scalar.activation(stat[:, 3:4], stat[:, 2:3], ACT.Sqrt).then_inc(q_act, 1)
            act.wait_ge(d_ln, 16 * (2 + NB * (2 + NQ)))
            act.wait_ge(q_pe, PE_W1 + KB)
            for m in range(KB):
                nc.scalar.activation(hmT[:, m, :], psB[:, NB * m:NB * (m + 1)], ACT.Gelu, bias=b1T[:, m:m + 1]).then_inc(q_act, 1)
            meet(act, "act")

            A = nc.scalar

            def body(_i, par, _known, w):
                def gates(h, s):
                    act.wait_ge(S[f"lstm_summed{h}"], s + 1)
                    A.activation(gate[h][:, :, :].rearrange("p g q -> p (g q)"), arg[h][:, :, :].rearrange("p g n -> p (g n)"),
                                 ACT.Tanh, scale=unscale[:, 1:2]).then_inc(S[f"lstm_gated{h}"], 1)

                def tanh_cell(h, s):
                    act.wait_ge(S[f"lstm_cell{h}"], s + 1)
                    A.activation(tc[h][:, :], cell[h][:, :], ACT.Tanh, scale=0.5).then_inc(S[f"lstm_tanhc{h}"], 1)

                for s in range(CT):
                    if w["lstm"]:
                        gates(0, s)
                        tanh_cell(0, s)
                        gates(1, s)
                        tanh_cell(1, s)
                    if w["rnn"]:
                        act.wait_ge(S["rnn_summed"], s + 1)
                        A.activation(hr[:, :, s, :], r_s2[:, :, :], ACT.Tanh).then_inc(S["rnn_tanh"], 1)

                    if w["l0"]:
                        if s == XT_STEP + 1:
                            act.wait_ge(S["xT_mm"], 1)
                            A.activation(xT[1 - par].rearrange("p b t n -> p b n t"),
                                         psX[:, :].rearrange("p (b n t) -> p b n t", b=KB, n=NB),
                                         ACT.Identity).then_inc(S["xT_ready"], 1)
                        if s == L0_STEP + KB:
                            act.wait_ge(S["l0_mm"], 1)
                            for m in range(KB):
                                A.activation(xr[1 - par][:, m, :, :],
                                             psI[:, TOK * m:TOK * (m + 1)].rearrange("p (t n) -> p t n", n=NB),
                                             ACT.Identity, bias=b_rnn[:, m:m + 1]).then_inc(S["l0_ready"], 1)
                    if w["mid"]:
                        if s < KB:
                            for k in range(TAPS):
                                A.activation(conv[:, s, :, :] if k == 0 else taps[k - 1][:, s, :, :], x1T[1 - par][:, s, k:k + CT, :],
                                             ACT.Identity, scale=condT[:, s, k:k + 1],
                                             bias=b_conv[:, s:s + 1] if k == 0 else 0.0).then_inc(S["tap_ready"], 1)
                        if s == WO_STEP + 1:
                            act.wait_ge(S["x2_ready"], 1)
                            A.activation(x2s[1 - par], x2[:, :, :, :], ACT.Copy, scale=2 * H_SCALE).then_inc(S["x2_scaled"], 1)
                        if s == SSM_STEP + 3:
                            act.wait_ge(S["ssm_mm"], 1)
                            A.activation(zabs[:, :], psS[0:NS, 0:TOK], ACT.Abs, bias=b_B[:, :]).then_inc(S["act_done"], 1)
                            A.activation(uu[:, :], psS[0:NS, 2 * TOK:3 * TOK], ACT.Identity, bias=b_u[:, :]).then_inc(S["ssm_out"], 1)
                            act.wait_ge(S["act_done"], 1)
                            A.activation(ez[:, :], zabs[:, :], ACT.Exp, scale=-1.0).then_inc(S["exp_ready"], 1)
                            A.activation(zmax[:, :], psS[0:NS, 0:TOK], ACT.Relu, bias=b_B[:, :]).then_inc(S["ssm_out"], 1)
                            A.activation(ct[:, :], psS[0:NS, TOK:2 * TOK], ACT.Tanh, bias=b_C[:, :]).then_inc(S["ssm_out"], 1)
                        if s == WO_STEP:
                            act.wait_ge(S["wo_mm"], 1)
                            for b in range(KB):
                                A.activation(x2[:, b, :, :], psX[:, TOK * b:TOK * (b + 1)].rearrange("p (t n) -> p t n", n=NB),
                                             ACT.Identity, bias=b_out[:, b:b + 1]).then_inc(S["wo_out"], 1)
                        for g in range(G):
                            if s == l2_last_step(g) + 1:
                                act.wait_ge(S["l2_mm"], g + 1)
                                ps = (psA, psB)[g % 2]
                                for b in range(KB):
                                    h, hb = b // HB, b % HB
                                    A.activation(
                                        xl[1 - par][:, :, h * HG + g * HB + hb, :],
                                        ps[:, TOK * b:TOK * (b + 1)].rearrange("p (t n) -> p t n", n=NB), ACT.Identity,
                                        bias=b_lsc[:, h, g, hb:hb + 1],
                                        scale=xscale[:, g // (G - 1):g // (G - 1) + 1]).then_inc(S["l2_ready"], 1)
                    if w["out"] and s == OUT_STEPS[-1] + 1:
                        act.wait_ge(S["out_mm"], 1)
                        A.activation(orow[:, :], psOut[:, :], ACT.Copy, scale=0.5 / H_SCALE).then_inc(S["out_ready"], 1)
                meet(act, "act")

            pipeline(act, body)

        @block.vector
        def _(vec):
            n = [0]

            def prep(ins, wait=True):
                n[0] += 1
                ins.then_inc(q_vec, 1)
                if wait:
                    vec.wait_ge(q_vec, n[0])

            V = nc.vector
            vec.wait_ge(d_rnnw, 16 * (3 + NB))
            prep(V.tensor_reduce(wmax[:, 0:1], whr32.rearrange("p k n -> p (k n)"), AX.X, ALU.max, apply_absolute_value=True))
            vec.wait_ge(q_pool, 1)

            def scales(e, hs):
                prep(V.tensor_scalar(wpow[:, e:e + 1], wmaxa[:, e:e + 1], 1e-18, None, ALU.max))
                prep(V.tensor_scalar(wpow[:, e:e + 1].bitcast(U32), wpow[:, e:e + 1].bitcast(U32), 0x7F800000, None, ALU.bitwise_and))
                prep(V.tensor_scalar(wscale[:, e:e + 1].bitcast(U32), wpow[:, e:e + 1].bitcast(U32), 0x7F800000, None, ALU.bitwise_xor))
                prep(V.tensor_scalar(wscale[:, e:e + 1], wscale[:, e:e + 1], 4096.0, None, ALU.mult))
                prep(V.tensor_scalar(unscale[:, e:e + 1], wpow[:, e:e + 1], 0.5 / 4096.0 / hs, None, ALU.mult))

            scales(0, R_SCALE)
            for k in range(KB):
                for m in range(KB):
                    src = whr32[:, k, P * m:P * (m + 1)]
                    hi, lo = (whr[:, k, e, m, :] for e in range(2))
                    prep(V.tensor_scalar(hi, src, wscale[:, 0:1], None, ALU.mult))
                    prep(V.scalar_tensor_tensor(out=lo, in0=src, scalar=wscale[:, 0:1], in1=hi, op0=ALU.mult, op1=ALU.subtract))
            for t in (hrs[:, :, :, :], hls[:, :, :], cell[0][:, :], cell[1][:, :], st0[:, :], x1T[0][:, :, :, :], psL0[:, :], psL1[:, :]):
                prep(V.memset(t, 0.0))
            vec.wait_ge(d_lstmw, 16)
            prep(V.tensor_reduce(wmax[:, 1:2], whl32.rearrange("p k n -> p (k n)"), AX.X, ALU.max, apply_absolute_value=True))
            assert n[0] == V_LMAX, n[0]
            vec.wait_ge(q_pool, 2)
            scales(1, H_SCALE)
            prep(V.tensor_scalar(xscale[:, 1:2], wscale[:, 1:2], H_SCALE, None, ALU.mult))
            prep(V.tensor_scalar(xscale[:, 0:1], wscale[:, 1:2], 0.5 * H_SCALE, None, ALU.mult))
            vec.wait_ge(q_pe, PE_H0)
            for k in range(KB):
                for g in range(G):
                    f = 0.5 if g < G - 1 else 1.0
                    f *= 0.5
                    src = whl32[:, k, g * D:(g + 1) * D]
                    prep(V.tensor_scalar(src, src, wscale[:, 1:2], f, ALU.mult, ALU.mult))
                    s4 = src.rearrange("p (h b j c) -> p h j b c", h=NH, b=HB, j=NQ)
                    for h in range(NH):
                        hi, lo = (whl[:, k, h, e, :, g * HB * QC:(g + 1) * HB * QC].rearrange("p j (b c) -> p j b c", b=HB)
                                  for e in range(2))
                        prep(V.tensor_copy(hi, s4[:, h]), wait=(h == 1))
                        if h == 1:
                            for h2 in range(NH):
                                hi2, lo2 = (whl[:, k, h2, e, :, g * HB * QC:(g + 1) * HB * QC].rearrange("p j (b c) -> p j b c", b=HB)
                                            for e in range(2))
                                prep(V.tensor_tensor(lo2, s4[:, h2], hi2, ALU.subtract), wait=(h2 == 1))
            assert n[0] == V_SPLIT, n[0]
            prep(V.tensor_copy(h0r[:, :, :], psR[:, 0:KB * NB].rearrange("p (m n) -> p m n", n=NB)))
            for g in range(G):
                prep(V.tensor_scalar(h0l[:, :, g, :, :],
                                     psR[:, 64 + g * KB * NB:64 + (g + 1) * KB * NB].rearrange("p (h b n) -> p h b n", h=NH, n=NB),
                                     xscale[:, g // (G - 1):g // (G - 1) + 1], None, ALU.mult))
            vec.wait_ge(d_small, 16 * 13)
            for g in range(G):
                prep(V.tensor_scalar(b_lsc[:, :, g, :], b_lstm[:, g * KB:(g + 1) * KB].rearrange("p (h b) -> p h b", h=NH),
                                     xscale[:, g // (G - 1):g // (G - 1) + 1], None, ALU.mult))
            prep(V.tensor_scalar(spw[:, 2, :], ab[:, :], 0.0, None, ALU.max))
            vec.wait_ge(q_act, A_EXP0)
            softplus(V, prep, spw[:, 2, :], spw[:, 1, :], spw[:, 3, :], spw[:, 3, :], spw[:, 4, :], spw[:, 5, :],
                     spw[:, 6, :], spw[:, 7, :], spt[:, :])
            prep(V.tensor_tensor(decay1[:, :], spt[:, 0:1], spt[:, 1:2], ALU.mult))
            prep(V.tensor_scalar(decay1[:, :], decay1[:, :], -1.0, 1.0, ALU.mult, ALU.add))
            prep(V.memset(decay[:, :], 1.0))
            prep(V.tensor_scalar(decay[:, :], decay[:, :], decay1[:, :], None, ALU.mult))
            vec.wait_ge(q_act, A_XR0)
            vec.wait_ge(d_ln, 16 * (2 + NB * (2 + NQ)))
            prep(V.reduce_sum(stat[:, 0:1], crow[:, :], axis=AX.X))
            prep(V.tensor_scalar(stat[:, 1:2], stat[:, 0:1], -1.0 / D, None, ALU.mult))
            prep(V.tensor_scalar(lnc[:, :], crow[:, :], stat[:, 1:2], None, ALU.add))
            prep(V.tensor_tensor(lnq[:, :], lnc[:, :], lnc[:, :], ALU.mult))
            prep(V.reduce_sum(stat[:, 4:5], lnq[:, :], axis=AX.X))
            prep(V.tensor_scalar(stat[:, 2:3], stat[:, 4:5], 1.0 / D, LN_EPS, ALU.mult, ALU.add))
            assert n[0] == V_LNVAR, n[0]
            vec.wait_ge(q_act, A_SQRT)
            prep(V.reciprocal(stat[:, 5:6], stat[:, 3:4]))
            prep(V.tensor_scalar(lnc[:, :], lnc[:, :], stat[:, 5:6], None, ALU.mult))
            prep(V.tensor_tensor(lnc[:, :], lnc[:, :], lng[:, :], ALU.mult))
            prep(V.tensor_tensor(ae, lnc[:, :], lnb[:, :], ALU.add))
            assert n[0] == V_AE, n[0]
            vec.wait_ge(q_pe, PE_AET)
            prep(V.tensor_copy(aeT[:, :, :], psS[:, 0:KB * NB].rearrange("p (k n) -> p k n", n=NB)))
            assert n[0] == V_AET, n[0]
            for q in range(W2R):
                vec.wait_ge(q_pe, PE_W2 + q + 1)
                for c in range(NQ):
                    src = (psA, psB)[q % 2][QC * c:QC * c + NB, 0:W2C // NQ].rearrange("p (d r) -> p r d", r=RANK)
                    add = b2s[QC * c:QC * c + NB, q, :].rearrange("p (d r) -> p r d", r=RANK)
                    prep(V.tensor_tensor(xw[QC * c:QC * c + NB, q, :, :], src, add, ALU.add), wait=False)
            vec.wait_ge(q_vec, n[0])
            assert n[0] == V_XW, n[0]
            vec.wait_ge(q_id, 2)
            for b in range(KB):
                d = baseI[:, b, P * b:P * (b + 1)]
                prep(V.scalar_tensor_tensor(out=d, in0=ident[:, :], scalar=2.0, in1=d, op0=ALU.mult, op1=ALU.add))
            for u in range(NB * KB):
                vec.wait_ge(q_pe, PE_LAYER + u + 1)
                prep(V.tensor_tensor(layer[:, u // KB, u % KB, :], (psA, psB)[u % 2][:, :], baseI[:, u % KB, :], ALU.add))
                assert n[0] == V_LAYER + u + 1, n[0]
            prep(V.tensor_tensor(xr[0][:, :, 0, :], xr[0][:, :, 0, :], h0r[:, :, :], ALU.add))
            meet(vec, "vec")

            def body(_i, par, _known, w):
                n = [0]

                def mark(ins):
                    n[0] += 1
                    ins.then_inc(S["vec_done"], 1)
                    return n[0]

                def half(t, h):
                    return t[:, h * HB:(h + 1) * HB]

                def transpose(h, s):
                    vec.wait_ge(S[f"lstm_mm{h}"], s + 1)
                    return mark(V.transpose(tr[h][s % 2][:, :, 0:QC], psL[h][:, 0:HW].rearrange("p (g c) -> p g c", c=QC)))

                def reduce(h, s, at):
                    vec.wait_ge(S[f"lstm_in_ready{h}"], s + 1)
                    vec.wait_ge(S["vec_done"], at)
                    three = tr[h][s % 2][:, :, :].rearrange("p g (s n) -> p g s n", n=NB)[:, :, 0:XS // NB + 1:LO // NB, :]
                    V.tensor_reduce(arg[h][:, :, :], three.rearrange("p g s n -> p g n s"), AX.X, ALU.add
                                    ).then_inc(S[f"lstm_summed{h}"], 1)

                def parts(h, s):
                    vec.wait_ge(S[f"lstm_gated{h}"], s + 1)
                    mark(V.scalar_tensor_tensor(out=c_f[h][:, :], in0=gate[h][:, 1, :], scalar=1.0, in1=cell[h][:, :],
                                                op0=ALU.add, op1=ALU.mult))
                    return mark(V.scalar_tensor_tensor(out=c_i[h][:, :], in0=gate[h][:, 0, :], scalar=1.0, in1=gate[h][:, 3, :],
                                                       op0=ALU.add, op1=ALU.mult))

                def new_cell(h, at):
                    vec.wait_ge(S["vec_done"], at)
                    V.scalar_tensor_tensor(out=cell[h][:, :], in0=c_f[h][:, :], scalar=0.5, in1=c_i[h][:, :],
                                           op0=ALU.mult, op1=ALU.add).then_inc(S[f"lstm_cell{h}"], 1)

                def out_gate(h):
                    return mark(V.tensor_scalar(o_s[h][:, :], gate[h][:, 2, :], 1.0, H_SCALE, ALU.add, ALU.mult))

                def new_h(h, s, o_at):
                    vec.wait_ge(S[f"lstm_tanhc{h}"], s + 1)
                    vec.wait_ge(S["vec_done"], o_at)
                    o3 = o_s[h][:, :].rearrange("p (b n) -> p b n", b=HB)
                    t3 = tc[h][:, :].rearrange("p (b n) -> p b n", b=HB)
                    mark(V.tensor_tensor(half(hl, h)[:, :, s, :], o3, t3, ALU.mult))
                    return mark(V.tensor_tensor(half(hls, h)[:, :, 0:NB], o3, t3, ALU.mult))

                def lo_part(h, s, at):
                    vec.wait_ge(S["vec_done"], at)
                    V.tensor_tensor(half(hls, h)[:, :, LO:LO + NB], half(hl, h)[:, :, s, :], half(hls, h)[:, :, 0:NB], ALU.subtract
                                    ).then_inc(S[f"lstm_h_ready{h}"], 1)

                def rnn_sum1(s):
                    vec.wait_ge(S["rnn_mm"], s + 1)
                    return mark(V.scalar_tensor_tensor(out=r_s1[:, :, :], in0=ps_rnn[:, :, 0, :], scalar=unscale[:, 0:1],
                                                       in1=xr[par][:, :, s, :], op0=ALU.mult, op1=ALU.add))

                def rnn_sum2(at):
                    vec.wait_ge(S["vec_done"], at)
                    V.scalar_tensor_tensor(out=r_s2[:, :, :], in0=ps_rnn[:, :, 1, :], scalar=unscale[:, 0:1],
                                           in1=r_s1[:, :, :], op0=ALU.mult, op1=ALU.add).then_inc(S["rnn_summed"], 1)

                for s in range(CT):
                    if w["lstm"]:
                        at = transpose(0, s)
                        reduce(0, s, at)
                        t_at = transpose(1, s)
                        at = parts(0, s)
                        new_cell(0, at)
                        o_at = out_gate(0)
                        reduce(1, s, t_at)
                        at = new_h(0, s, o_at)
                        lo_part(0, s, at)
                        at = parts(1, s)
                        new_cell(1, at)
                        o_at = out_gate(1)
                    if w["rnn"]:
                        r_at = rnn_sum1(s)
                    if w["lstm"]:
                        at = new_h(1, s, o_at)
                    if w["rnn"]:
                        rnn_sum2(r_at)
                    if w["lstm"]:
                        lo_part(1, s, at)
                    if w["rnn"]:
                        vec.wait_ge(S["rnn_tanh"], s + 1)
                        at = mark(V.tensor_scalar(hrs[:, :, 0, :], hr[:, :, s, :], R_SCALE, None, ALU.mult))
                        vec.wait_ge(S["vec_done"], at)
                        V.scalar_tensor_tensor(out=hrs[:, :, 1, :], in0=hr[:, :, s, :], scalar=R_SCALE, in1=hrs[:, :, 0, :],
                                               op0=ALU.mult, op1=ALU.subtract).then_inc(S["rnn_h_ready"], 1)

                    if w["mid"]:
                        if s == SSM_STEP + 3:
                            vec.wait_ge(S["den_ready"], 1)
                            V.reciprocal(rden[:, :], den[:, :]).then_inc(S["recip_ready"], 1)
                        if s == SCAN_STEP:
                            vec.wait_ge(S["drive_ready"], 1)
                            dv = drive[:, :].rearrange("p (t n) -> p t n", n=NB)
                            for b in range(NB):
                                at = mark(V.tensor_tensor_scan(states[:, :, b], decay[:, :], dv[:, :, b], st0[:, b:b + 1], ALU.mult, ALU.add))
                            vec.wait_ge(S["vec_done"], at)
                            V.tensor_copy(st0[:, :], states[:, CT - 1, :]).then_inc(S["scan_ready"], 1)
                meet(vec, "vec")

            pipeline(vec, body)

        @block.tensor
        def _(pe):
            mm = nc.tensor.matmul
            pe.wait_ge(d_rnnw, 16 * (3 + NB))
            for m in range(KB):
                for k in range(KB):
                    w_ = whr32[:, k, P * m:P * (m + 1)]
                    mm(psR[:, NB * m:NB * (m + 1)], w_, condT[:, k, :], start=(k == 0), stop=(k == KB - 1))
            pe.wait_ge(q_id, 2)
            pe.wait_ge(d_x0, 16)
            for b in range(KB):
                last = x_transpose(mm, xrow, psX, ident, b)
            last.then_inc(q_pe, 1)
            pe.wait_ge(q_act, A_XT0)
            for m in range(KB):
                for k in range(KB):
                    last = rnn_in(mm, wxr, xT[0], psI, m, k)
                last.then_inc(q_pe, 1)
            pe.wait_ge(d_lstmw, 16)
            for g in range(G):
                for m in range(KB):
                    for k in range(KB):
                        w_ = whl32[:, k, g * D + P * m:g * D + P * (m + 1)]
                        o = 64 + (g * KB + m) * NB
                        last = mm(psR[:, o:o + NB], w_, condT[:, k, :], start=(k == 0), stop=(k == KB - 1))
            last.then_inc(q_pe, 1)
            pe.wait_ge(q_vec, V_AE)
            for k in range(KB):
                last = mm(psS[:, NB * k:NB * (k + 1)], ae[:, P * k:P * (k + 1)], ident[0:NB, 0:NB], start=True, stop=True)
            last.then_inc(q_pe, 1)
            pe.wait_ge(q_vec, V_AET)
            pe.wait_ge(d_w1, 16)
            for m in range(KB):
                for k in range(KB):
                    last = mm(psB[:, NB * m:NB * (m + 1)], w1s[:, k, P * m:P * (m + 1)], aeT[:, k, :], start=(k == 0), stop=(k == KB - 1))
                last.then_inc(q_pe, 1)
            pe.wait_ge(q_act, A_GELU)
            for q in range(W2R):
                pe.wait_ge(d_w2[q % 2], 16 * (q // 2 + 1))
                if q >= 2:
                    pe.wait_ge(q_vec, V_AET + NQ * (q - 1))
                wd = W2C // NQ
                for k in range(KB):
                    for c in range(NQ):
                        last = mm((psA, psB)[q % 2][QC * c:QC * c + NB, 0:wd], hmT[:, k, :], w2s[q % 2][:, k, wd * c:wd * (c + 1)],
                                  start=(k == 0), stop=(k == KB - 1), tile_position=(0, QC * c))
                last.then_inc(q_pe, 1)
            pe.wait_ge(d_xab, 16 * 2 * NQ * NB * (W2R // 2))
            pe.wait_ge(q_vec, V_XW)
            for u in range(NB * KB):
                if u >= 2:
                    pe.wait_ge(q_vec, V_LAYER + u - 1)
                w_ = xab[:, u // KB, P * (u % KB):P * (u % KB + 1)]
                mm((psA, psB)[u % 2][:, :], w_, xbb[:, u // KB, :], start=True, stop=True).then_inc(q_pe, 1)
            meet(pe, "pe")

            def body(_i, par, _known, w):
                for s in range(CT):
                    if w["lstm"]:
                        def products(h, k, parts=(0, 1)):
                            for e in parts:
                                for j in range(NQ):
                                    ins = mm(psL[h][QC * j:QC * j + LO + NB, 0:HW], hls[:, k, :], whl[:, k, h, e, j, :],
                                             start=(k == 0 and e == 0), stop=(k == KB - 1 and e == 1), tile_position=(0, QC * j))
                            return ins

                        if s > 0:
                            pe.wait_ge(S["lstm_h_ready0"], s)
                        products(0, 0)
                        products(0, 1)
                        products(1, 0, (0,))
                        if s > 0:
                            pe.wait_ge(S["lstm_h_ready1"], s)
                        products(0, 2)
                        products(0, 3).then_inc(S["lstm_mm0"], 1)
                        products(1, 0, (1,))
                        products(1, 1)
                        products(1, 2)
                        products(1, 3).then_inc(S["lstm_mm1"], 1)
                    if w["rnn"]:
                        if s > 0:
                            pe.wait_ge(S["rnn_h_ready"], s)
                        for m in range(KB):
                            for k in range(KB):
                                for e in range(2):
                                    last = mm(psR[:, m * 2 * NB:(m + 1) * 2 * NB], whr[:, k, e, m, :],
                                              hrs[:, k, :, :].rearrange("p s n -> p (s n)"),
                                              start=(k == 0 and e == 0), stop=(k == KB - 1 and e == 1))
                        last.then_inc(S["rnn_mm"], 1)

                    if w["out"] and s in OUT_STEPS:
                        k = OUT_STEPS.index(s)
                        for n in range(NB):
                            last = mm(psOut[CT * n:CT * (n + 1), :], x3s[1 - par][:, k, :, n], layer[:, n, k, :],
                                      start=(k == 0), stop=(k == KB - 1), tile_position=(0, CT * n))
                        if k == KB - 1:
                            last.then_inc(S["out_mm"], 1)
                    if w["l0"] and s == XT_STEP:
                        for b in range(KB):
                            last = x_transpose(mm, xrow, psX, ident, b)
                        last.then_inc(S["xT_mm"], 1)
                    if w["mid"] and SSM_STEP <= s < SSM_STEP + 3:
                        c = s - SSM_STEP
                        if c == 0:
                            pe.wait_ge(S["conv_ready"], KB)
                        for k in range(KB):
                            w_ = wp[:, k, NS * c:NS * (c + 1)] if c < 2 else ws[:, k, :]
                            r_ = conv[:, k, :, :] if c < 2 else x1T[1 - par][:, k, HALO:HALO + CT, :]
                            last = mm(psS[0:NS, TOK * c:TOK * (c + 1)], w_, r_.rearrange("p t n -> p (t n)"),
                                      start=(k == 0), stop=(k == KB - 1))
                        if c == 2:
                            last.then_inc(S["ssm_mm"], 1)
                    if w["l0"] and L0_STEP <= s < L0_STEP + KB:
                        if s == L0_STEP:
                            pe.wait_ge(S["xT_ready"], 1)
                        for k in range(KB):
                            last = rnn_in(mm, wxr, xT[1 - par], psI, s - L0_STEP, k)
                        if s == L0_STEP + KB - 1:
                            last.then_inc(S["l0_mm"], 1)
                    if w["mid"] and s == WO_STEP:
                        pe.wait_ge(S["y_ready"], 1)
                        for b in range(KB):
                            w_ = wo[:, P * b:P * (b + 1)]
                            last = mm(psX[:, TOK * b:TOK * (b + 1)], w_, y[:, :], start=True, stop=True)
                        last.then_inc(S["wo_mm"], 1)
                    if w["mid"] and s >= L2_STEP:
                        for u in range(L2_MM * (s - L2_STEP), min(L2_MM * (s - L2_STEP + 1), L2_ALL)):
                            g, b, k = u // (KB * KB), u // KB % KB, u % KB
                            if u == 0:
                                pe.wait_ge(S["x2_ready"], 1)
                                if w["l0"]:
                                    pe.wait_ge(S["l0_ready"], KB)
                            if g >= 2 and b == 0 and k == 0:
                                pe.wait_ge(S["l2_ready"], KB * (g - 1))
                            w_ = wxl[:, k, g * D + P * b:g * D + P * (b + 1)]
                            last = mm((psA, psB)[g % 2][:, TOK * b:TOK * (b + 1)], w_, x2[:, k, :, :].rearrange("p t n -> p (t n)"),
                                      start=(k == 0), stop=(k == KB - 1))
                            if b == KB - 1 and k == KB - 1:
                                last.then_inc(S["l2_mm"], 1)
                meet(pe, "pe")

            pipeline(pe, body)


def x_transpose(mm, xrow, psX, ident, b):
    w_ = xrow[:, P * b:P * (b + 1)]
    return mm(psX[:, TOK * b:TOK * (b + 1)], w_, ident[:, :], start=True, stop=True)


def rnn_in(mm, wxr, xT, psI, m, k):
    w_ = wxr[:, k, P * m:P * (m + 1)]
    return mm(psI[:, TOK * m:TOK * (m + 1)], w_, xT[:, k, :, :].rearrange("p t n -> p (t n)"),
              start=(k == 0), stop=(k == KB - 1))


def softplus(V, link, zmax, ez, den, rden, s, q, pa, pb_, out):
    link(V.tensor_scalar(den, ez, 2.0, None, ALU.add))
    link(V.reciprocal(rden, den))
    link(V.tensor_tensor(s, ez, rden, ALU.mult))
    link(V.tensor_tensor(q, s, s, ALU.mult))
    link(V.tensor_scalar(pa, q, 1.0 / 15, None, ALU.mult))
    link(V.scalar_tensor_tensor(out=pb_, in0=pa, scalar=1.0 / 13, in1=q, op0=ALU.add, op1=ALU.mult))
    link(V.scalar_tensor_tensor(out=pa, in0=pb_, scalar=1.0 / 11, in1=q, op0=ALU.add, op1=ALU.mult))
    link(V.scalar_tensor_tensor(out=pb_, in0=pa, scalar=1.0 / 9, in1=q, op0=ALU.add, op1=ALU.mult))
    link(V.scalar_tensor_tensor(out=pa, in0=pb_, scalar=1.0 / 7, in1=q, op0=ALU.add, op1=ALU.mult))
    link(V.scalar_tensor_tensor(out=pb_, in0=pa, scalar=1.0 / 5, in1=q, op0=ALU.add, op1=ALU.mult))
    link(V.scalar_tensor_tensor(out=pa, in0=pb_, scalar=1.0 / 3, in1=q, op0=ALU.add, op1=ALU.mult))
    link(V.scalar_tensor_tensor(out=pb_, in0=pa, scalar=1.0, in1=s, op0=ALU.add, op1=ALU.mult))
    link(V.scalar_tensor_tensor(out=out, in0=pb_, scalar=2.0, in1=zmax, op0=ALU.mult, op1=ALU.add))


V_RSPLIT = 1 + 5 + 2 * KB * KB
V_LMAX = V_RSPLIT + 8 + 1
V_SPLIT = V_LMAX + 7 + 5 * KB * G
V_DECAY = V_SPLIT + 1 + G + G + 1 + 13 + 4
V_LNVAR = V_DECAY + 6
V_AE = V_LNVAR + 4
V_AET = V_AE + 1
V_XW = V_AET + W2R * NQ
V_LAYER = V_XW + KB
PE_X0 = 1
PE_H0 = PE_X0 + KB + 1
PE_AET = PE_H0 + 1
PE_W1 = PE_AET
PE_W2 = PE_W1 + KB
PE_LAYER = PE_W2 + W2R
A_XT0 = 1
A_XR0 = A_XT0 + KB
A_EXP0 = A_XR0 + 2
A_SQRT = A_EXP0 + 1
A_GELU = A_SQRT + KB

_INS = ['x', 'cond_1024', 'L0_cond_Wx', 'L0_cond_Wh', 'L0_cond_b', 'L1_cond_conv_b', 'L1_cond_Wp', 'L1_cond_bp',
        'L1_cond_Ws', 'L1_cond_bs', 'L1_cond_A_log', 'L1_cond_dt_log', 'L1_cond_Wo', 'L1_cond_bo', 'L2_cond_Wx',
        'L2_cond_Wh', 'L2_cond_b', 'L3_cond_base_layer', 'L3_cond_w1', 'L3_cond_b1', 'L3_cond_w2', 'L3_cond_b2',
        'L3_cond_ln_g', 'L3_cond_ln_b']


def kernel(**inputs):
    import concourse.bacc as bacc
    from concourse.bass_utils import run_bass_kernel_spmd

    nc = bacc.Bacc("TRN2", target_bir_lowering=False, num_devices=1)
    arrays, args = {}, []
    for name in _INS:
        a = np.ascontiguousarray(inputs[name])
        arrays[f"in_{name}"] = a
        args.append(nc.dram_tensor(f"in_{name}", a.shape, mybir.dt.from_np(a.dtype), kind="ExternalInput").ap())
    out = nc.dram_tensor("out_0", (NB, T, D), F32, kind="ExternalOutput").ap()
    resid_stack_kernel(nc, *args, out)
    r = run_bass_kernel_spmd(nc, [arrays], core_ids=[0])
    return r.results[0]["out_0"]
```

```python
import numpy as np
import concourse.bass as bass
from concourse import mybir
from contextlib import ExitStack

F32 = mybir.dt.float32
F16 = mybir.dt.float16
U32 = mybir.dt.uint32
ALU = mybir.AluOpType
ACT = mybir.ActivationFunctionType
AX = mybir.AxisListType
RMAX = bass.bass_isa.ReduceOp.max

P = 128
NB, T, D = 4, 1024, 512
CT = 32
NCH = T // CT
TOK = NB * CT
KB = D // P
QC = 32
NQ = P // QC
G = 4
GB = G * KB
NS = 64
TAPS = 4
RANK = 8
LN_EPS = 1e-5
H_SCALE = 4096.0
R_SCALE = 8192.0
NH = 2
HB = KB // NH
HG = G * HB
HW = HG * QC
LO = 16
XS = 2 * LO
PIECES = [(0, 14), (14, 24), (24, 30), (30, 32)]
W2C = 1024
W2R = 2 * D * RANK // W2C
DP = W2C // NQ // RANK

XT_STEP = 0
OUT_STEPS = [1, 2, 6, 13]
CONV_STEPS = [0, 1, 2, 2]
SSM_STEP = 3
HOLD_STEPS = [11, 30, 31]
L0_STEP = 7
RECIP_STEP = 7
RECIP_CUTS = [0, 40, 88, TOK]
SCAN_STEP = 11
WO_STEP = 12
ARRIVE_STEP = 20
L2_STEP = 14
L2_MM = 4
L2_ALL = GB * KB


def l2_last_step(g):
    return L2_STEP + (KB * KB * (g + 1) - 1) // L2_MM


def chunk_work(i):
    return dict(rnn=0 <= i < NCH, l0=i >= 0 and i + 1 < NCH, l0_after=i >= 0 and i + 2 < NCH, mid=1 <= i <= NCH,
                lstm=2 <= i <= NCH + 1, out=3 <= i <= NCH + 2)


FIRST_FULL, LAST_FULL = 4, NCH - 3
assert (LAST_FULL + 1 - FIRST_FULL) % 2 == 0
HEAD = list(range(0, FIRST_FULL))
TAIL = list(range(LAST_FULL + 1, NCH + 3))


def resid_stack_kernel(nc, x, cond, l0_Wx, l0_Wh, l0_b, conv_b, Wp, bp, Ws, bs, A_log, dt_log, Wo, bo,
                       l2_Wx, l2_Wh, l2_b, base, w1, b1, w2, b2, ln_g, ln_b, out):
    ctx = ExitStack()
    with ctx:
        def sb(name, shape, dt=F32):
            return ctx.enter_context(nc.sbuf_tensor(name, shape, dt))

        def pb(name):
            return ctx.enter_context(nc.psum_tensor(name, [P, 512], F32))

        def sem(name):
            return ctx.enter_context(nc.semaphore(name))

        stage = sb("stage", [P, 5 * 2048])

        def reuse(at):
            return stage[:, at * KB * TOK:(at + 1) * KB * TOK]

        whl = sb("lstm_Wh_parts", [P, KB, NH, 2, NQ, HW], F16)
        whr = sb("rnn_Wh_parts", [P, KB, 2, KB, P], F16)
        wxl = sb("lstm_Wx", [P, KB, G * D])
        wxr = sb("rnn_Wx", [P, KB, D])
        wp = sb("ssm_Wp", [P, KB, 2 * NS])
        ws = sb("ssm_Ws", [P, KB, NS])
        wo = sb("ssm_Wo", [NS, D])
        layer = sb("layer_plus_2I", [P, NB, KB, D])
        condT = sb("condT", [P, KB, NB])
        b_rnn = sb("b_rnn", [P, KB])
        b_lstm = sb("b_lstm", [P, GB])
        b_lsc = sb("b_lstm_scaled", [P, NH, G, HB])
        b_conv = sb("b_conv", [P, KB])
        b_out = sb("b_ssm_out", [P, KB])
        b_B = sb("b_B", [NS, 1])
        b_C = sb("b_C", [NS, 1])
        b_u = sb("b_u", [NS, 1])
        ab = sb("A_dt_log", [NS, 2])
        spt = sb("softplus_A_dt", [NS, 2])
        decay = sb("decay", [NS, CT])
        decay1 = sb("decay1", [NS, 1])
        ident = sb("ident", [P, P])
        wmax = sb("wmax", [P, 2])
        wmaxa = sb("wmaxa", [P, 2])
        wpow = sb("wpow", [P, 2])
        wscale = sb("wscale", [P, 2])
        unscale = sb("unscale", [P, 2])
        xscale = sb("lstm_in_scale", [P, 2])
        h0r = sb("h0_rnn", [P, KB, NB])
        h0l = sb("h0_lstm", [P, NH, G, HB, NB])
        def hidden(v):
            return v.rearrange("p (b t n) -> p b t n", b=KB, t=CT)

        HALO = TAPS - 1
        xrow = sb("x_rows", [P, D])
        xT = [sb("xT_0", [P, KB, CT, NB])[:, :, :, :], hidden(reuse(0))]
        xr = [sb("rnn_in_0", [P, KB, CT, NB])[:, :, :, :], hidden(reuse(1))]
        hr = sb("rnn_h", [P, KB, CT, NB])
        x1T = [sb(f"x1T_{e}", [P, KB, HALO + CT, NB]) for e in range(2)]
        x2 = sb("x2", [P, KB, CT, NB])
        x2s = [sb("x2_scaled_0", [P, KB, CT, NB])[:, :, :, :], hidden(reuse(2))]
        xl = [sb(f"lstm_in_{e}", [P, CT, GB, NB]) for e in range(2)]
        hl = sb("lstm_h_scaled", [P, KB, CT, NB])
        x3s = [sb("x3_scaled_0", [P, KB, CT, NB])[:, :, :, :], hidden(reuse(8))]
        orow = sb("out_rows", [P, D])
        hrs = sb("rnn_h_parts", [P, KB, 2, NB], F16)
        hls = sb("lstm_h_parts", [P, KB, LO + NB], F16)
        r_s1 = sb("rnn_sum1", [P, KB, NB])
        r_s2 = sb("rnn_sum2", [P, KB, NB])
        tr = [[sb(f"lstm_sums_{h}{e}", [P, HG, XS + NB]) for e in range(2)] for h in range(NH)]
        arg = [sb(f"lstm_arg{h}", [P, HG, NB]) for h in range(NH)]
        gate = [sb(f"lstm_gates{h}", [P, G, HB * NB]) for h in range(NH)]
        cell = [sb(f"lstm_2c{h}", [P, HB * NB]) for h in range(NH)]
        c_f = [sb(f"lstm_f_part{h}", [P, HB * NB]) for h in range(NH)]
        c_i = [sb(f"lstm_i_part{h}", [P, HB * NB]) for h in range(NH)]
        o_s = [sb(f"lstm_o_scaled{h}", [P, HB * NB]) for h in range(NH)]
        tc = [sb(f"lstm_tanh_c{h}", [P, HB * NB]) for h in range(NH)]
        conv = hidden(reuse(3))
        taps = [hidden(reuse(9 + k)) for k in range(TAPS - 1)]
        zabs, zmax, ez, uu, den, rden, sr, qr, bt, ct, drive, y, pol_a, pol_b, st_ = [
            stage[:, 4 * 512 + TOK * q:4 * 512 + TOK * (q + 1)] for q in range(15)]
        zabs, zmax, ez, uu, den, rden, sr, qr, bt, ct, drive, y, pol_a, pol_b, st_ = [
            v[0:NS, :] for v in (zabs, zmax, ez, uu, den, rden, sr, qr, bt, ct, drive, y, pol_a, pol_b, st_)]
        states = st_.rearrange("p (t n) -> p t n", n=NB)
        st0 = sb("state0", [NS, NB])
        spw = sb("softplus_work", [NS, 8, 2])
        whl32 = stage[:, 0:8192].rearrange("p (k n) -> p k n", k=KB)
        whr32 = stage[:, 8192:10240].rearrange("p (k n) -> p k n", k=KB)
        w1s = whr32
        w2s = [stage[:, h * 4096:(h + 1) * 4096].rearrange("p (k n) -> p k n", k=KB) for h in range(2)]
        b2s = xl[1][:, :, :, :].rearrange("p t g n -> p (t g n)").rearrange("p (q n) -> p q n", q=W2R)
        xw = xl[0][:, :, :, :].rearrange("p t g n -> p (t g n)").rearrange("p (e r a d) -> p e r a d", e=2, r=RANK, d=DP)
        xab = stage[0:RANK, 8192:10240].rearrange("p (n d) -> p n d", n=NB)
        xbb = stage[0:RANK, 0:2048].rearrange("p (n d) -> p n d", n=NB)
        baseI = layer[:, NB - 1, :, :]
        ae = orow[0:NB, :]
        crow, lng, lnb, lnc, lnq = [t[0:NB, :, :, :].rearrange("p b t n -> p (b t n)") for t in (x2, x2s[0], x3s[0], hl, hr)]
        stat = sb("ln_stat", [NB, 8])
        aeT = sb("aeT", [P, KB, NB])
        hmT = sb("hmT", [P, KB, NB])
        b1T = sb("b1T", [P, KB])

        psL0, psL1, psR, psOut, psX, psS, psA, psB = [pb(n) for n in
            ("ps_lstm0", "ps_lstm1", "ps_rnn", "ps_out", "ps_x", "ps_ssm", "ps_lstm_in_a", "ps_lstm_in_b")]
        psL = (psL0, psL1)
        psI = psA
        ps_rnn = psR[:, 0:KB * 2 * NB].rearrange("p (m s n) -> p m s n", m=KB, s=2)

        d_rnnw, d_x0, d_lstmw, d_small, d_w1, d_w2a, d_w2b, d_xab, d_ln = [sem(n) for n in
            ("d_rnnw", "d_x0", "d_lstmw", "d_small", "d_w1", "d_w2a", "d_w2b", "d_xab", "d_ln")]
        d_w2 = [d_w2a, d_w2b]
        q_id, q_zero, q_vec, q_pool, q_pe, q_act = [sem(n) for n in
            ("q_id", "q_zero", "q_vec", "q_pool", "q_pe", "q_act")]
        arrive = sem("engines_arrived")
        x_arrived = sem("x_arrived")
        go = {e: sem(f"go_{e}") for e in ("pe", "act", "vec", "pool")}
        names = [f"{n}{h}" for h in range(NH) for n in ("lstm_mm", "lstm_summed", "lstm_gated", "lstm_cell", "lstm_tanhc",
                                                        "lstm_h_ready", "lstm_in_ready")]
        names += ["rnn_mm", "rnn_summed", "rnn_tanh", "rnn_h_ready", "vec_done", "pool_done", "act_done",
                  "den_ready", "tap_ready", "xT_mm", "xT_ready", "l0_mm", "l0_ready", "conv_ready", "ssm_mm", "ssm_out", "exp_ready", "recip_ready",
                  "drive_ready", "scan_ready", "y_ready", "wo_mm", "wo_out",
                  "x2_ready", "l2_mm", "l2_ready", "out_mm", "out_ready", "out_stored", "x1_ready", "x3_ready", "next_x_arrived"]
        sets = [{n: sem(f"{n}_{e}") for n in names} for e in range(2)]
        set_range = []
        for e in range(2):
            nums = sorted(s.num for s in sets[e].values())
            assert nums == list(range(nums[0], nums[0] + len(nums)))
            set_range.append(range(nums[0], nums[-1] + 1))

        block = ctx.enter_context(nc.Block())

        def rows(w):
            return w.rearrange("(k p) n -> p k n", p=P)

        def column(v):
            return v.rearrange("(k p) -> p k", p=P)

        def pipeline(eng, body):
            for i in HEAD:
                body(i, i % 2, i, chunk_work(i), chunk_work(i - 1))
            with eng.Fori(FIRST_FULL, LAST_FULL, 2) as i:
                for h in range(2):
                    body(i + h, (FIRST_FULL + h) % 2, None, chunk_work(FIRST_FULL + h), chunk_work(FIRST_FULL + 1))
            for i in TAIL:
                body(i, i % 2, i, chunk_work(i), chunk_work(i - 1))

        def meet(eng, name):
            eng.drain().then_inc(arrive, 1)
            eng.wait_ge(go[name], 1)
            eng.sem_clear(go[name])

        def next_chunk(eng, name):
            eng.wait_ge(go[name], 1)
            eng.sem_clear(go[name])

        @block.sync
        def _(sp):
            x_v = x.rearrange("n (i t) d -> i n t d", t=CT)
            out_v = out.rearrange("n (i t) d -> i n t d", t=CT)
            with nc.allow_non_contiguous_dma("weights in hidden layout"):
                sp.dma_start(whr32, rows(l0_Wh)).then_inc(d_rnnw, 16)
                sp.dma_start(wxr[:, :, :], rows(l0_Wx)).then_inc(d_rnnw, 16)
                for n in range(NB):
                    sp.dma_start(condT[:, :, n], column(cond[n])).then_inc(d_rnnw, 16)
                sp.dma_start(b_rnn[:, :], column(l0_b)).then_inc(d_rnnw, 16)
                sp.dma_start(xrow[:, :], x_v[0]).then_inc(d_x0, 16)
                row = lambda v: v.rearrange("(o n) -> o n", o=1)
                sp.dma_start(crow[:, :], cond[:, :]).then_inc(d_ln, 16)
                for n in range(NB):
                    sp.dma_start(lng[n:n + 1, :], row(ln_g)).then_inc(d_ln, 16)
                    sp.dma_start(lnb[n:n + 1, :], row(ln_b)).then_inc(d_ln, 16)
                    for q in range(NQ):
                        src = b2.rearrange("(a q g d) -> a q g d", a=1, g=NQ, d=W2C // NQ)[:, :, q, :]
                        sp.dma_start(b2s[QC * q + n:QC * q + n + 1, :, :], src).then_inc(d_ln, 16)
                sp.dma_start(b1T[:, :], column(b1)).then_inc(d_ln, 16)
                sp.dma_start(whl32, rows(l2_Wh)).then_inc(d_lstmw, 16)
                sp.wait_ge(q_vec, V_RSPLIT)
                sp.wait_ge(q_pe, PE_X0)
                sp.dma_start(w1s, rows(w1)).then_inc(d_w1, 16)
                cut = lambda v, a: v[a:a + NS].rearrange("(p o) -> p o", o=1)
                for dst, src in ((b_lstm[:, :], column(l2_b)), (b_conv[:, :], column(conv_b)), (b_out[:, :], column(bo)),
                                 (b_B[:, :], cut(bp, 0)), (b_C[:, :], cut(bp, NS)), (b_u[:, :], cut(bs, 0)),
                                 (ab[:, 0:1], cut(A_log, 0)), (ab[:, 1:2], cut(dt_log, 0)),
                                 (wp[:, :, :], rows(Wp)), (ws[:, :, :], rows(Ws)), (wo[:, :], Wo[:, :]),
                                 (wxl[:, :, :], rows(l2_Wx)), (baseI, rows(base))):
                    sp.dma_start(dst, src).then_inc(d_small, 16)
                sp.wait_ge(q_vec, V_SPLIT)
                sp.wait_ge(q_pe, PE_H0)
                w2v = w2.rearrange("(k p) (q n) -> q p k n", p=P, n=W2C)
                for q in range(W2R):
                    if q >= 2:
                        sp.wait_ge(q_pe, PE_W2 + q - 1)
                    sp.dma_start(w2s[q % 2], w2v[q]).then_inc(d_w2[q % 2], 16)
                sp.wait_ge(q_vec, V_XW)
                for half, dst in ((0, xab), (1, xbb)):
                    for q in range(NQ):
                        for n in range(NB):
                            sp.dma_start(dst[:, n, :].rearrange("r (a q d) -> r a q d", q=NQ, d=DP)[:, :, q, :],
                                         xw[QC * q + n:QC * q + n + 1, half, :, :, :]
                                         ).then_inc(d_xab, 16)

            def body(i, par, _known, w, _p):
                S = sets[par]
                if w["l0_after"]:
                    sp.wait_ge(S["xT_mm"], 1)
                    sp.dma_start(xrow[:, :], x_v[i + 2]).then_inc(S["next_x_arrived"], 16)
                if w["out"]:
                    sp.wait_ge(S["out_ready"], 1)
                    for n in range(NB):
                        sp.dma_start(out_v[i - 3, n], orow[CT * n:CT * (n + 1), :]).then_inc(S["out_stored"], 16)
                    sp.wait_ge(S["out_stored"], 16 * NB)
                sp.wait_ge(arrive, 4)
                sp.sem_clear(set_range[1 - par])
                sp.sem_clear(arrive)
                for e in go.values():
                    sp.sem_inc(e, 1)

            sp.wait_ge(q_pe, PE_X0)
            sp.dma_start(xrow[:, :], x_v[1]).then_inc(x_arrived, 16)
            sp.wait_ge(x_arrived, 16)
            sp.wait_ge(arrive, 4)
            sp.sem_clear(arrive)
            for e in go.values():
                sp.sem_inc(e, 1)
            pipeline(sp, body)

        @block.gpsimd
        def _(pool):
            nc.gpsimd.memset(ident[:, :], 0.0).then_inc(q_id, 1)
            pool.wait_ge(q_id, 1)
            nc.gpsimd.affine_select(out=ident[:, :], in_=ident[:, :], compare_op=ALU.not_equal, fill=1.0, base=0,
                                    pattern=[[-1, P]], channel_multiplier=1).then_inc(q_id, 1)
            pool.wait_ge(q_vec, 1)
            nc.gpsimd.partition_all_reduce(wmaxa[:, 0:1], wmax[:, 0:1], P, RMAX).then_inc(q_pool, 1)
            pool.wait_ge(q_vec, V_LMAX)
            nc.gpsimd.partition_all_reduce(wmaxa[:, 1:2], wmax[:, 1:2], P, RMAX).then_inc(q_pool, 1)
            meet(pool, "pool")

            def body(_i, par, known, w, p):
                S, S_last = sets[par], sets[1 - par]
                n = [0]

                def step(ins):
                    n[0] += 1
                    ins.then_inc(S["pool_done"], 1)
                    pool.wait_ge(S["pool_done"], n[0])

                Q = nc.gpsimd

                def fill(s):
                    for h in range(NH):
                        if s >= 2:
                            pool.wait_ge(S[f"lstm_summed{h}"], s - 1)
                        elif p["lstm"]:
                            pool.wait_ge(S_last[f"lstm_summed{h}"], CT - 1 + s)
                        Q.tensor_copy(tr[h][s % 2][:, :, XS:XS + NB],
                                      xl[par][:, s, h * HG:(h + 1) * HG, :]).then_inc(S[f"lstm_in_ready{h}"], 1)

                def convolve(b):
                    pool.wait_ge(S["tap_ready"], TAPS * (b + 1))
                    for k in range(1, TAPS):
                        ins = Q.tensor_tensor(conv[:, b, :, :], conv[:, b, :, :], taps[k - 1][:, b, :, :], ALU.add)
                        if k < TAPS - 1:
                            step(ins)
                    ins.then_inc(S["conv_ready"], 1)

                def series(c, last=False):
                    step(Q.tensor_scalar(pol_b, pol_a, c, None, ALU.add))
                    step(Q.tensor_tensor(pol_a, pol_b, sr if last else qr, ALU.mult))

                def residuals(a, z, par=par, w=w, S=S):
                    ts = slice(a, z)
                    if w["rnn"]:
                        pool.wait_ge(S["rnn_tanh"], z)
                        Q.tensor_tensor(x1T[par][:, :, HALO + a:HALO + z, :], xT[par][:, :, ts, :], hr[:, :, ts, :], ALU.add
                                        ).then_inc(S["x1_ready"], 1)
                    if w["lstm"]:
                        for h in range(NH):
                            pool.wait_ge(S[f"lstm_h_ready{h}"], z)
                        Q.tensor_tensor(x3s[par][:, :, ts, :], x2s[par][:, :, ts, :], hl[:, :, ts, :], ALU.add
                                        ).then_inc(S["x3_ready"], 1)

                if w["lstm"]:
                    pool.wait_ge(S_last["l2_ready"], GB)
                if known == 2:
                    step(Q.tensor_tensor(xl[par][:, 0, :, :], xl[par][:, 0, :, :],
                                         h0l[:, :, :, :, :].rearrange("p h g b n -> p (h g b) n"), ALU.add))
                if w["lstm"]:
                    fill(0)
                    fill(1)
                if p["rnn"] or p["lstm"]:
                    residuals(*PIECES[-1], par=1 - par, w=p, S=S_last)
                for s in range(CT):
                    if w["lstm"] and s + 2 < CT:
                        fill(s + 2)
                    if s == ARRIVE_STEP:
                        pool.sem_inc(arrive, 1)
                    if w["mid"]:
                        for b in range(KB):
                            if s == CONV_STEPS[b]:
                                convolve(b)
                        if s == SSM_STEP + 3:
                            pool.wait_ge(S["exp_ready"], 1)
                            Q.tensor_scalar(den[:, :], ez[:, :], 2.0, None, ALU.add).then_inc(S["den_ready"], 1)
                        if s == SSM_STEP + 4:
                            pool.wait_ge(S["recip_ready"], len(RECIP_CUTS) - 1)
                            step(Q.tensor_tensor(sr[:, :], ez[:, :], rden[:, :], ALU.mult))
                            step(Q.tensor_tensor(qr[:, :], sr[:, :], sr[:, :], ALU.mult))
                            step(Q.tensor_scalar(pol_a, qr[:, :], 1.0 / 15, None, ALU.mult))
                        if s == SSM_STEP + 5:
                            for c in (13, 11, 9, 7, 5):
                                series(1.0 / c)
                        if s == SSM_STEP + 6:
                            pool.wait_ge(S["ssm_out"], 3)
                            step(Q.tensor_scalar(drive[:, :], uu[:, :], spt[:, 1:2], None, ALU.mult))
                            series(1.0 / 3)
                            series(1.0, last=True)
                            step(Q.tensor_scalar(pol_b, pol_a, 2.0, None, ALU.mult))
                            step(Q.tensor_tensor(bt[:, :], pol_b, zmax[:, :], ALU.add))
                            Q.tensor_tensor(drive[:, :], drive[:, :], bt[:, :], ALU.mult).then_inc(S["drive_ready"], 1)
                        if s == SCAN_STEP:
                            pool.wait_ge(S["scan_ready"], 1)
                            Q.tensor_tensor(y[:, :], states[:, :, :].rearrange("p t n -> p (t n)"), ct[:, :], ALU.mult
                                            ).then_inc(S["y_ready"], 1)
                        if s == WO_STEP + 1:
                            pool.wait_ge(S["wo_out"], KB)
                            Q.tensor_tensor(x2[:, :, :, :], x2[:, :, :, :], x1T[1 - par][:, :, HALO:HALO + CT, :], ALU.add
                                            ).then_inc(S["x2_ready"], 1)
                    if w["rnn"] and w["mid"] and s == PIECES[0][1]:
                        pool.wait_ge(S_last["x1_ready"], len(PIECES))
                        step(Q.tensor_copy(x1T[par][:, :, 0:HALO, :], x1T[1 - par][:, :, CT:CT + HALO, :]))
                    for a, z in PIECES:
                        if s == z:
                            residuals(a, z)
                next_chunk(pool, "pool")

            pipeline(pool, body)

        @block.scalar
        def _(act):
            act.wait_ge(q_pe, PE_X0)
            nc.scalar.activation(xT[0].rearrange("p b t n -> p b n t"),
                                 psX[:, :].rearrange("p (b n t) -> p b n t", b=KB, n=NB), ACT.Identity).then_inc(q_act, 1)
            act.wait_ge(q_pe, PE_X0 + KB)
            for m in range(KB):
                nc.scalar.activation(xr[0][:, m, :, :], psI[:, TOK * m:TOK * (m + 1)].rearrange("p (t n) -> p t n", n=NB),
                                     ACT.Identity, bias=b_rnn[:, m:m + 1]).then_inc(q_act, 1)
            act.wait_ge(q_vec, V_LNVAR)
            nc.scalar.activation(stat[:, 3:4], stat[:, 2:3], ACT.Sqrt).then_inc(q_act, 1)
            act.wait_ge(d_ln, 16 * (2 + NB * (2 + NQ)))
            act.wait_ge(q_pe, PE_W1 + KB)
            for m in range(KB):
                nc.scalar.activation(hmT[:, m, :], psB[:, NB * m:NB * (m + 1)], ACT.Gelu, bias=b1T[:, m:m + 1]).then_inc(q_act, 1)
            act.wait_ge(d_small, 16 * 13)
            nc.scalar.activation(spw[:, 0, :], ab[:, :], ACT.Abs).then_inc(q_act, 1)
            act.wait_ge(q_act, A_GELU + 1)
            nc.scalar.activation(spw[:, 1, :], spw[:, 0, :], ACT.Exp, scale=-1.0).then_inc(q_act, 1)
            meet(act, "act")

            A = nc.scalar

            def body(_i, par, _known, w, p):
                S, S_last = sets[par], sets[1 - par]
                def gates(h, s):
                    act.wait_ge(S[f"lstm_summed{h}"], s + 1)
                    A.activation(gate[h][:, :, :].rearrange("p g q -> p (g q)"), arg[h][:, :, :].rearrange("p g n -> p (g n)"),
                                 ACT.Tanh, scale=unscale[:, 1:2]).then_inc(S[f"lstm_gated{h}"], 1)

                def tanh_cell(h, s):
                    act.wait_ge(S[f"lstm_cell{h}"], s + 1)
                    A.activation(tc[h][:, :], cell[h][:, :], ACT.Tanh, scale=0.5).then_inc(S[f"lstm_tanhc{h}"], 1)

                def conv_taps(a, z):
                    for u in range(a, z):
                        b, k = u // TAPS, u % TAPS
                        A.activation(conv[:, b, :, :] if k == 0 else taps[k - 1][:, b, :, :], x1T[1 - par][:, b, k:k + CT, :],
                                     ACT.Identity, scale=condT[:, b, k:k + 1],
                                     bias=b_conv[:, b:b + 1] if k == 0 else 0.0).then_inc(S["tap_ready"], 1)

                for s in range(CT):
                    for h in range(NH):
                        if w["lstm"]:
                            gates(h, s)
                        if w["mid"] and 1 <= s < KB:
                            conv_taps(TAPS * s + TAPS // NH * h, TAPS * s + TAPS // NH * (h + 1))
                        if w["lstm"]:
                            tanh_cell(h, s)
                    if s == 0 and p["rnn"]:
                        act.wait_ge(S_last["x1_ready"], len(PIECES))
                    if w["rnn"]:
                        act.wait_ge(S["rnn_summed"], s + 1)
                        A.activation(hr[:, :, s, :], r_s2[:, :, :], ACT.Tanh).then_inc(S["rnn_tanh"], 1)
                    if s == ARRIVE_STEP:
                        act.sem_inc(arrive, 1)

                    if w["l0"]:
                        if s == XT_STEP + 3:
                            act.wait_ge(S["xT_mm"], 1)
                            A.activation(xT[1 - par].rearrange("p b t n -> p b n t"),
                                         psX[:, :].rearrange("p (b n t) -> p b n t", b=KB, n=NB),
                                         ACT.Identity).then_inc(S["xT_ready"], 1)
                        if s == L0_STEP + KB:
                            act.wait_ge(S["l0_mm"], 1)
                            for m in range(KB):
                                A.activation(xr[1 - par][:, m, :, :],
                                             psI[:, TOK * m:TOK * (m + 1)].rearrange("p (t n) -> p t n", n=NB),
                                             ACT.Identity, bias=b_rnn[:, m:m + 1]).then_inc(S["l0_ready"], 1)
                    if w["mid"]:
                        if s == 0:
                            conv_taps(0, TAPS)
                        if s == WO_STEP + 1:
                            act.wait_ge(S["x2_ready"], 1)
                            A.activation(x2s[1 - par], x2[:, :, :, :], ACT.Copy, scale=2 * H_SCALE)
                        if s == SSM_STEP + 3:
                            act.wait_ge(S["ssm_mm"], 1)
                            A.activation(zabs[:, :], psS[0:NS, 0:TOK], ACT.Abs, bias=b_B[:, :]).then_inc(S["act_done"], 1)
                            act.wait_ge(S["act_done"], 1)
                            A.activation(ez[:, :], zabs[:, :], ACT.Exp, scale=-1.0).then_inc(S["exp_ready"], 1)
                        if s == SSM_STEP + 4:
                            A.activation(uu[:, :], psS[0:NS, 2 * TOK:3 * TOK], ACT.Identity, bias=b_u[:, :]).then_inc(S["ssm_out"], 1)
                            A.activation(zmax[:, :], psS[0:NS, 0:TOK], ACT.Relu, bias=b_B[:, :]).then_inc(S["ssm_out"], 1)
                        if s == SSM_STEP + 5:
                            A.activation(ct[:, :], psS[0:NS, TOK:2 * TOK], ACT.Tanh, bias=b_C[:, :]).then_inc(S["ssm_out"], 1)
                        if s == WO_STEP:
                            act.wait_ge(S["wo_mm"], 1)
                            for b in range(KB):
                                A.activation(x2[:, b, :, :], psX[:, TOK * b:TOK * (b + 1)].rearrange("p (t n) -> p t n", n=NB),
                                             ACT.Identity, bias=b_out[:, b:b + 1]).then_inc(S["wo_out"], 1)
                        for g in range(G):
                            if s == l2_last_step(g) + 1:
                                act.wait_ge(S["l2_mm"], g + 1)
                                ps = (psA, psB)[g % 2]
                                for b in range(KB):
                                    h, hb = b // HB, b % HB
                                    A.activation(
                                        xl[1 - par][:, :, h * HG + g * HB + hb, :],
                                        ps[:, TOK * b:TOK * (b + 1)].rearrange("p (t n) -> p t n", n=NB), ACT.Identity,
                                        bias=b_lsc[:, h, g, hb:hb + 1],
                                        scale=xscale[:, g // (G - 1):g // (G - 1) + 1]).then_inc(S["l2_ready"], 1)
                    if w["out"] and s == OUT_STEPS[-1] + 1:
                        act.wait_ge(S["out_mm"], 1)
                        if p["out"]:
                            act.wait_ge(S_last["out_stored"], 16 * NB)
                        A.activation(orow[:, :], psOut[:, :], ACT.Copy, scale=0.5 / H_SCALE).then_inc(S["out_ready"], 1)
                next_chunk(act, "act")

            pipeline(act, body)

        @block.vector
        def _(vec):
            n = [0]

            def prep(ins, wait=True):
                n[0] += 1
                ins.then_inc(q_vec, 1)
                if wait:
                    vec.wait_ge(q_vec, n[0])

            V = nc.vector
            vec.wait_ge(d_rnnw, 16 * (3 + NB))
            prep(V.tensor_reduce(wmax[:, 0:1], whr32.rearrange("p k n -> p (k n)"), AX.X, ALU.max, apply_absolute_value=True))
            vec.wait_ge(q_pool, 1)

            def scales(e, hs):
                prep(V.tensor_scalar(wpow[:, e:e + 1], wmaxa[:, e:e + 1], 1e-18, None, ALU.max))
                prep(V.tensor_scalar(wpow[:, e:e + 1].bitcast(U32), wpow[:, e:e + 1].bitcast(U32), 0x7F800000, None, ALU.bitwise_and))
                prep(V.tensor_scalar(wscale[:, e:e + 1].bitcast(U32), wpow[:, e:e + 1].bitcast(U32), 0x7F800000, None, ALU.bitwise_xor))
                prep(V.tensor_scalar(wscale[:, e:e + 1], wscale[:, e:e + 1], 4096.0, None, ALU.mult))
                prep(V.tensor_scalar(unscale[:, e:e + 1], wpow[:, e:e + 1], 0.5 / 4096.0 / hs, None, ALU.mult))

            scales(0, R_SCALE)
            for k in range(KB):
                for m in range(KB):
                    src = whr32[:, k, P * m:P * (m + 1)]
                    hi, lo = (whr[:, k, e, m, :] for e in range(2))
                    prep(V.tensor_scalar(hi, src, wscale[:, 0:1], None, ALU.mult))
                    prep(V.scalar_tensor_tensor(out=lo, in0=src, scalar=wscale[:, 0:1], in1=hi, op0=ALU.mult, op1=ALU.subtract))
            for t in (hrs[:, :, :, :], hls[:, :, :], cell[0][:, :], cell[1][:, :], st0[:, :], x1T[0][:, :, :, :], psL0[:, :], psL1[:, :]):
                prep(V.memset(t, 0.0))
            vec.wait_ge(d_ln, 16 * (2 + NB * (2 + NQ)))
            prep(V.reduce_sum(stat[:, 0:1], crow[:, :], axis=AX.X))
            prep(V.tensor_scalar(stat[:, 1:2], stat[:, 0:1], -1.0 / D, None, ALU.mult))
            prep(V.tensor_scalar(lnc[:, :], crow[:, :], stat[:, 1:2], None, ALU.add))
            prep(V.tensor_tensor(lnq[:, :], lnc[:, :], lnc[:, :], ALU.mult))
            prep(V.reduce_sum(stat[:, 4:5], lnq[:, :], axis=AX.X))
            prep(V.tensor_scalar(stat[:, 2:3], stat[:, 4:5], 1.0 / D, LN_EPS, ALU.mult, ALU.add))
            assert n[0] == V_LNVAR, n[0]
            vec.wait_ge(q_act, A_SQRT)
            prep(V.reciprocal(stat[:, 5:6], stat[:, 3:4]))
            prep(V.tensor_scalar(lnc[:, :], lnc[:, :], stat[:, 5:6], None, ALU.mult))
            prep(V.tensor_tensor(lnc[:, :], lnc[:, :], lng[:, :], ALU.mult))
            prep(V.tensor_tensor(ae, lnc[:, :], lnb[:, :], ALU.add))
            assert n[0] == V_AE, n[0]
            vec.wait_ge(q_pe, PE_AET)
            prep(V.tensor_copy(aeT[:, :, :], psS[:, 0:KB * NB].rearrange("p (k n) -> p k n", n=NB)))
            assert n[0] == V_AET, n[0]
            vec.wait_ge(d_lstmw, 16)
            prep(V.tensor_reduce(wmax[:, 1:2], whl32.rearrange("p k n -> p (k n)"), AX.X, ALU.max, apply_absolute_value=True))
            assert n[0] == V_LMAX, n[0]
            vec.wait_ge(q_pool, 2)
            scales(1, H_SCALE)
            prep(V.tensor_scalar(xscale[:, 1:2], wscale[:, 1:2], H_SCALE, None, ALU.mult))
            prep(V.tensor_scalar(xscale[:, 0:1], wscale[:, 1:2], 0.5 * H_SCALE, None, ALU.mult))
            vec.wait_ge(q_pe, PE_H0)
            for k in range(KB):
                for g in range(G):
                    f = 0.5 if g < G - 1 else 1.0
                    f *= 0.5
                    src = whl32[:, k, g * D:(g + 1) * D]
                    prep(V.tensor_scalar(src, src, wscale[:, 1:2], f, ALU.mult, ALU.mult))
                    s4 = src.rearrange("p (h b j c) -> p h j b c", h=NH, b=HB, j=NQ)
                    for h in range(NH):
                        hi, lo = (whl[:, k, h, e, :, g * HB * QC:(g + 1) * HB * QC].rearrange("p j (b c) -> p j b c", b=HB)
                                  for e in range(2))
                        prep(V.tensor_copy(hi, s4[:, h]), wait=(h == 1))
                        if h == 1:
                            for h2 in range(NH):
                                hi2, lo2 = (whl[:, k, h2, e, :, g * HB * QC:(g + 1) * HB * QC].rearrange("p j (b c) -> p j b c", b=HB)
                                            for e in range(2))
                                prep(V.tensor_tensor(lo2, s4[:, h2], hi2, ALU.subtract), wait=(h2 == 1))
            assert n[0] == V_SPLIT, n[0]
            prep(V.tensor_copy(h0r[:, :, :], psR[:, 0:KB * NB].rearrange("p (m n) -> p m n", n=NB)))
            for g in range(G):
                prep(V.tensor_scalar(h0l[:, :, g, :, :],
                                     psR[:, 64 + g * KB * NB:64 + (g + 1) * KB * NB].rearrange("p (h b n) -> p h b n", h=NH, n=NB),
                                     xscale[:, g // (G - 1):g // (G - 1) + 1], None, ALU.mult))
            vec.wait_ge(d_small, 16 * 13)
            for g in range(G):
                prep(V.tensor_scalar(b_lsc[:, :, g, :], b_lstm[:, g * KB:(g + 1) * KB].rearrange("p (h b) -> p h b", h=NH),
                                     xscale[:, g // (G - 1):g // (G - 1) + 1], None, ALU.mult))
            prep(V.tensor_scalar(spw[:, 2, :], ab[:, :], 0.0, None, ALU.max))
            vec.wait_ge(q_act, A_EXP0)
            softplus(V, prep, spw[:, 2, :], spw[:, 1, :], spw[:, 3, :], spw[:, 3, :], spw[:, 4, :], spw[:, 5, :],
                     spw[:, 6, :], spw[:, 7, :], spt[:, :])
            prep(V.tensor_tensor(decay1[:, :], spt[:, 0:1], spt[:, 1:2], ALU.mult))
            prep(V.tensor_scalar(decay1[:, :], decay1[:, :], -1.0, 1.0, ALU.mult, ALU.add))
            prep(V.memset(decay[:, :], 1.0))
            prep(V.tensor_scalar(decay[:, :], decay[:, :], decay1[:, :], None, ALU.mult))
            vec.wait_ge(q_act, A_XR0)
            for q in range(W2R):
                vec.wait_ge(q_pe, PE_W2 + q + 1)
                for c in range(NQ):
                    src = (psA, psB)[q % 2][QC * c:QC * c + NB, 0:W2C // NQ].rearrange("p (d r) -> p r d", r=RANK)
                    add = b2s[QC * c:QC * c + NB, q, :].rearrange("p (d r) -> p r d", r=RANK)
                    prep(V.tensor_tensor(xw[QC * c:QC * c + NB, q // (W2R // 2), :, q % (W2R // 2), :], src, add, ALU.add), wait=False)
            vec.wait_ge(q_vec, n[0])
            assert n[0] == V_XW, n[0]
            vec.wait_ge(q_id, 2)
            for b in range(KB):
                d = baseI[:, b, P * b:P * (b + 1)]
                prep(V.scalar_tensor_tensor(out=d, in0=ident[:, :], scalar=2.0, in1=d, op0=ALU.mult, op1=ALU.add))
            for u in range(NB * KB):
                vec.wait_ge(q_pe, PE_LAYER + u + 1)
                prep(V.tensor_tensor(layer[:, u // KB, u % KB, :], (psA, psB)[u % 2][:, :], baseI[:, u % KB, :], ALU.add))
                assert n[0] == V_LAYER + u + 1, n[0]
            prep(V.tensor_tensor(xr[0][:, :, 0, :], xr[0][:, :, 0, :], h0r[:, :, :], ALU.add))
            meet(vec, "vec")

            def body(_i, par, _known, w, p):
                S, S_last = sets[par], sets[1 - par]
                n = [0]

                def mark(ins):
                    n[0] += 1
                    ins.then_inc(S["vec_done"], 1)
                    return n[0]

                def half(t, h):
                    return t[:, h * HB:(h + 1) * HB]

                def transpose(h, s):
                    vec.wait_ge(S[f"lstm_mm{h}"], s + 1)
                    return mark(V.transpose(tr[h][s % 2][:, :, 0:QC], psL[h][:, 0:HW].rearrange("p (g c) -> p g c", c=QC)))

                def reduce(h, s, at):
                    vec.wait_ge(S[f"lstm_in_ready{h}"], s + 1)
                    vec.wait_ge(S["vec_done"], at)
                    three = tr[h][s % 2][:, :, :].rearrange("p g (s n) -> p g s n", n=NB)[:, :, 0:XS // NB + 1:LO // NB, :]
                    V.tensor_reduce(arg[h][:, :, :], three.rearrange("p g s n -> p g n s"), AX.X, ALU.add
                                    ).then_inc(S[f"lstm_summed{h}"], 1)

                def parts(h, s):
                    vec.wait_ge(S[f"lstm_gated{h}"], s + 1)
                    mark(V.scalar_tensor_tensor(out=c_f[h][:, :], in0=gate[h][:, 1, :], scalar=1.0, in1=cell[h][:, :],
                                                op0=ALU.add, op1=ALU.mult))
                    return mark(V.scalar_tensor_tensor(out=c_i[h][:, :], in0=gate[h][:, 0, :], scalar=1.0, in1=gate[h][:, 3, :],
                                                       op0=ALU.add, op1=ALU.mult))

                def new_cell(h, at):
                    vec.wait_ge(S["vec_done"], at)
                    V.scalar_tensor_tensor(out=cell[h][:, :], in0=c_f[h][:, :], scalar=0.5, in1=c_i[h][:, :],
                                           op0=ALU.mult, op1=ALU.add).then_inc(S[f"lstm_cell{h}"], 1)

                def out_gate(h):
                    return mark(V.tensor_scalar(o_s[h][:, :], gate[h][:, 2, :], 1.0, H_SCALE, ALU.add, ALU.mult))

                def new_h(h, s, o_at):
                    vec.wait_ge(S[f"lstm_tanhc{h}"], s + 1)
                    vec.wait_ge(S["vec_done"], o_at)
                    o3 = o_s[h][:, :].rearrange("p (b n) -> p b n", b=HB)
                    t3 = tc[h][:, :].rearrange("p (b n) -> p b n", b=HB)
                    mark(V.tensor_tensor(half(hl, h)[:, :, s, :], o3, t3, ALU.mult))
                    return mark(V.tensor_tensor(half(hls, h)[:, :, 0:NB], o3, t3, ALU.mult))

                def lo_part(h, s, at):
                    vec.wait_ge(S["vec_done"], at)
                    V.tensor_tensor(half(hls, h)[:, :, LO:LO + NB], half(hl, h)[:, :, s, :], half(hls, h)[:, :, 0:NB], ALU.subtract
                                    ).then_inc(S[f"lstm_h_ready{h}"], 1)

                def ssm_stage(s, part):
                    if s == RECIP_STEP:
                        if part == 0:
                            vec.wait_ge(S["den_ready"], 1)
                        cut = slice(RECIP_CUTS[part], RECIP_CUTS[part + 1])
                        V.reciprocal(rden[:, cut], den[:, cut]).then_inc(S["recip_ready"], 1)
                    if s == SCAN_STEP and part < 2:
                        if part == 0:
                            vec.wait_ge(S["drive_ready"], 1)
                        dv = drive[:, :].rearrange("p (t n) -> p t n", n=NB)
                        for b in range(NB // 2 * part, NB // 2 * (part + 1)):
                            at = mark(V.tensor_tensor_scan(states[:, :, b], decay[:, :], dv[:, :, b], st0[:, b:b + 1], ALU.mult, ALU.add))
                        if part == 1:
                            vec.wait_ge(S["vec_done"], at)
                            V.tensor_copy(st0[:, :], states[:, CT - 1, :]).then_inc(S["scan_ready"], 1)

                def rnn_sum1(s):
                    if s == 0 and p["l0"]:
                        vec.wait_ge(S_last["l0_ready"], KB)
                    vec.wait_ge(S["rnn_mm"], s + 1)
                    return mark(V.scalar_tensor_tensor(out=r_s1[:, :, :], in0=ps_rnn[:, :, 0, :], scalar=unscale[:, 0:1],
                                                       in1=xr[par][:, :, s, :], op0=ALU.mult, op1=ALU.add))

                def rnn_sum2(at):
                    vec.wait_ge(S["vec_done"], at)
                    V.scalar_tensor_tensor(out=r_s2[:, :, :], in0=ps_rnn[:, :, 1, :], scalar=unscale[:, 0:1],
                                           in1=r_s1[:, :, :], op0=ALU.mult, op1=ALU.add).then_inc(S["rnn_summed"], 1)

                for s in range(CT):
                    if s == ARRIVE_STEP:
                        vec.sem_inc(arrive, 1)
                    if w["mid"] and not w["lstm"]:
                        ssm_stage(s, 0)
                        ssm_stage(s, 1)
                    if w["lstm"]:
                        at = transpose(0, s)
                        reduce(0, s, at)
                        if w["mid"]:
                            ssm_stage(s, 0)
                        t_at = transpose(1, s)
                        at = parts(0, s)
                        new_cell(0, at)
                        o_at = out_gate(0)
                        reduce(1, s, t_at)
                        at = new_h(0, s, o_at)
                        lo_part(0, s, at)
                        at = parts(1, s)
                        new_cell(1, at)
                        o_at = out_gate(1)
                        if w["mid"]:
                            ssm_stage(s, 1)
                        at = new_h(1, s, o_at)
                        lo_part(1, s, at)
                    if w["rnn"]:
                        rnn_sum2(rnn_sum1(s))
                        vec.wait_ge(S["rnn_tanh"], s + 1)
                        at = mark(V.tensor_scalar(hrs[:, :, 0, :], hr[:, :, s, :], R_SCALE, None, ALU.mult))
                        vec.wait_ge(S["vec_done"], at)
                        V.scalar_tensor_tensor(out=hrs[:, :, 1, :], in0=hr[:, :, s, :], scalar=R_SCALE, in1=hrs[:, :, 0, :],
                                               op0=ALU.mult, op1=ALU.subtract).then_inc(S["rnn_h_ready"], 1)
                    if w["mid"] and s == RECIP_STEP:
                        ssm_stage(s, 2)
                next_chunk(vec, "vec")

            pipeline(vec, body)

        @block.tensor
        def _(pe):
            mm = nc.tensor.matmul
            pe.wait_ge(d_rnnw, 16 * (3 + NB))
            for m in range(KB):
                for k in range(KB):
                    w_ = whr32[:, k, P * m:P * (m + 1)]
                    mm(psR[:, NB * m:NB * (m + 1)], w_, condT[:, k, :], start=(k == 0), stop=(k == KB - 1))
            pe.wait_ge(q_id, 2)
            pe.wait_ge(d_x0, 16)
            for b in range(KB):
                last = x_transpose(mm, xrow, psX, ident, b)
            last.then_inc(q_pe, 1)
            pe.wait_ge(q_act, A_XT0)
            for m in range(KB):
                for k in range(KB):
                    last = rnn_in(mm, wxr, xT[0], psI, m, k)
                last.then_inc(q_pe, 1)
            pe.wait_ge(q_vec, V_AE)
            for k in range(KB):
                last = mm(psS[:, NB * k:NB * (k + 1)], ae[:, P * k:P * (k + 1)], ident[0:NB, 0:NB], start=True, stop=True)
            last.then_inc(q_pe, 1)
            pe.wait_ge(q_vec, V_AET)
            pe.wait_ge(d_w1, 16)
            for m in range(KB):
                for k in range(KB):
                    last = mm(psB[:, NB * m:NB * (m + 1)], w1s[:, k, P * m:P * (m + 1)], aeT[:, k, :], start=(k == 0), stop=(k == KB - 1))
                last.then_inc(q_pe, 1)
            pe.wait_ge(d_lstmw, 16)
            for g in range(G):
                for m in range(KB):
                    for k in range(KB):
                        w_ = whl32[:, k, g * D + P * m:g * D + P * (m + 1)]
                        o = 64 + (g * KB + m) * NB
                        last = mm(psR[:, o:o + NB], w_, condT[:, k, :], start=(k == 0), stop=(k == KB - 1))
            last.then_inc(q_pe, 1)
            pe.wait_ge(q_act, A_GELU)
            for q in range(W2R):
                pe.wait_ge(d_w2[q % 2], 16 * (q // 2 + 1))
                if q >= 2:
                    pe.wait_ge(q_vec, V_DECAY + NQ * (q - 1))
                wd = W2C // NQ
                for k in range(KB):
                    for c in range(NQ):
                        last = mm((psA, psB)[q % 2][QC * c:QC * c + NB, 0:wd], hmT[:, k, :], w2s[q % 2][:, k, wd * c:wd * (c + 1)],
                                  start=(k == 0), stop=(k == KB - 1), tile_position=(0, QC * c))
                last.then_inc(q_pe, 1)
            pe.wait_ge(d_xab, 16 * 2 * NQ * NB)
            pe.wait_ge(q_vec, V_XW)
            for u in range(NB * KB):
                if u >= 2:
                    pe.wait_ge(q_vec, V_LAYER + u - 1)
                w_ = xab[:, u // KB, P * (u % KB):P * (u % KB + 1)]
                mm((psA, psB)[u % 2][:, :], w_, xbb[:, u // KB, :], start=True, stop=True).then_inc(q_pe, 1)
            meet(pe, "pe")

            def body(_i, par, _known, w, p):
                S, S_last = sets[par], sets[1 - par]
                for s in range(CT):
                    if s == ARRIVE_STEP:
                        pe.sem_inc(arrive, 1)
                    if w["lstm"]:
                        def products(h, k, parts=(0, 1)):
                            for e in parts:
                                for j in range(NQ):
                                    ins = mm(psL[h][QC * j:QC * j + LO + NB, 0:HW], hls[:, k, :], whl[:, k, h, e, j, :],
                                             start=(k == 0 and e == 0), stop=(k == KB - 1 and e == 1), tile_position=(0, QC * j))
                            return ins

                        if s == 0 and p["lstm"]:
                            pe.wait_ge(S_last["lstm_h_ready0"], CT)
                        elif s > 0:
                            pe.wait_ge(S["lstm_h_ready0"], s)
                        products(0, 0)
                        products(0, 1)
                        products(1, 0)
                        if s == 0 and p["lstm"]:
                            pe.wait_ge(S_last["lstm_h_ready1"], CT)
                        elif s > 0:
                            pe.wait_ge(S["lstm_h_ready1"], s)
                        products(0, 2)
                        products(0, 3).then_inc(S["lstm_mm0"], 1)
                        products(1, 1)
                        products(1, 2)
                        products(1, 3).then_inc(S["lstm_mm1"], 1)
                    if w["rnn"]:
                        if s == 0 and p["rnn"]:
                            pe.wait_ge(S_last["rnn_h_ready"], CT)
                        elif s > 0:
                            pe.wait_ge(S["rnn_h_ready"], s)
                        for m in range(KB):
                            for k in range(KB):
                                for e in range(2):
                                    last = mm(psR[:, m * 2 * NB:(m + 1) * 2 * NB], whr[:, k, e, m, :],
                                              hrs[:, k, :, :].rearrange("p s n -> p (s n)"),
                                              start=(k == 0 and e == 0), stop=(k == KB - 1 and e == 1))
                        last.then_inc(S["rnn_mm"], 1)

                    if w["out"] and s in OUT_STEPS:
                        k = OUT_STEPS.index(s)
                        if k == 0:
                            pe.wait_ge(S_last["x3_ready"], len(PIECES))
                            if p["out"]:
                                pe.wait_ge(S_last["out_ready"], 1)
                        for n in range(NB):
                            last = mm(psOut[CT * n:CT * (n + 1), :], x3s[1 - par][:, k, :, n], layer[:, n, k, :],
                                      start=(k == 0), stop=(k == KB - 1), tile_position=(0, CT * n))
                        if k == KB - 1:
                            last.then_inc(S["out_mm"], 1)
                    if w["l0"] and s == XT_STEP:
                        if p["l0_after"]:
                            pe.wait_ge(S_last["next_x_arrived"], 16)
                        for b in range(KB):
                            last = x_transpose(mm, xrow, psX, ident, b)
                        last.then_inc(S["xT_mm"], 1)
                    if w["mid"] and SSM_STEP <= s < SSM_STEP + 3:
                        c = (2, 0, 1)[s - SSM_STEP]
                        if c == 2:
                            pe.wait_ge(S_last["x1_ready"], len(PIECES))
                        if c == 0:
                            pe.wait_ge(S["conv_ready"], KB)
                        for k in range(KB):
                            w_ = wp[:, k, NS * c:NS * (c + 1)] if c < 2 else ws[:, k, :]
                            r_ = conv[:, k, :, :] if c < 2 else x1T[1 - par][:, k, HALO:HALO + CT, :]
                            last = mm(psS[0:NS, TOK * c:TOK * (c + 1)], w_, r_.rearrange("p t n -> p (t n)"),
                                      start=(k == 0), stop=(k == KB - 1))
                        if c == 1:
                            last.then_inc(S["ssm_mm"], 1)
                    if w["l0"] and L0_STEP <= s < L0_STEP + KB:
                        if s == L0_STEP:
                            pe.wait_ge(S["xT_ready"], 1)
                            if p["mid"]:
                                pe.wait_ge(S_last["l2_ready"], GB)
                        for k in range(KB):
                            last = rnn_in(mm, wxr, xT[1 - par], psI, s - L0_STEP, k)
                        if s == L0_STEP + KB - 1:
                            last.then_inc(S["l0_mm"], 1)
                    if s in HOLD_STEPS:
                        for _ in range(3):
                            mm(psS[:, 3 * TOK:4 * TOK], ident[:, :], ident[:, :], start=True, stop=True)
                    if w["mid"] and s == WO_STEP:
                        pe.wait_ge(S["y_ready"], 1)
                        for b in range(KB):
                            w_ = wo[:, P * b:P * (b + 1)]
                            last = mm(psX[:, TOK * b:TOK * (b + 1)], w_, y[:, :], start=True, stop=True)
                        last.then_inc(S["wo_mm"], 1)
                    if w["mid"] and s >= L2_STEP:
                        for u in range(L2_MM * (s - L2_STEP), min(L2_MM * (s - L2_STEP + 1), L2_ALL)):
                            g, b, k = u // (KB * KB), u // KB % KB, u % KB
                            if u == 0:
                                pe.wait_ge(S["x2_ready"], 1)
                                if p["mid"]:
                                    pe.wait_ge(S_last["l2_ready"], GB)
                                if w["l0"]:
                                    pe.wait_ge(S["l0_ready"], KB)
                            if g >= 2 and b == 0 and k == 0:
                                pe.wait_ge(S["l2_ready"], KB * (g - 1))
                            w_ = wxl[:, k, g * D + P * b:g * D + P * (b + 1)]
                            last = mm((psA, psB)[g % 2][:, TOK * b:TOK * (b + 1)], w_, x2[:, k, :, :].rearrange("p t n -> p (t n)"),
                                      start=(k == 0), stop=(k == KB - 1))
                            if b == KB - 1 and k == KB - 1:
                                last.then_inc(S["l2_mm"], 1)
                next_chunk(pe, "pe")

            pipeline(pe, body)


def x_transpose(mm, xrow, psX, ident, b):
    w_ = xrow[:, P * b:P * (b + 1)]
    return mm(psX[:, TOK * b:TOK * (b + 1)], w_, ident[:, :], start=True, stop=True)


def rnn_in(mm, wxr, xT, psI, m, k):
    w_ = wxr[:, k, P * m:P * (m + 1)]
    return mm(psI[:, TOK * m:TOK * (m + 1)], w_, xT[:, k, :, :].rearrange("p t n -> p (t n)"),
              start=(k == 0), stop=(k == KB - 1))


def softplus(V, link, zmax, ez, den, rden, s, q, pa, pb_, out):
    link(V.tensor_scalar(den, ez, 2.0, None, ALU.add))
    link(V.reciprocal(rden, den))
    link(V.tensor_tensor(s, ez, rden, ALU.mult))
    link(V.tensor_tensor(q, s, s, ALU.mult))
    link(V.tensor_scalar(pa, q, 1.0 / 15, None, ALU.mult))
    link(V.scalar_tensor_tensor(out=pb_, in0=pa, scalar=1.0 / 13, in1=q, op0=ALU.add, op1=ALU.mult))
    link(V.scalar_tensor_tensor(out=pa, in0=pb_, scalar=1.0 / 11, in1=q, op0=ALU.add, op1=ALU.mult))
    link(V.scalar_tensor_tensor(out=pb_, in0=pa, scalar=1.0 / 9, in1=q, op0=ALU.add, op1=ALU.mult))
    link(V.scalar_tensor_tensor(out=pa, in0=pb_, scalar=1.0 / 7, in1=q, op0=ALU.add, op1=ALU.mult))
    link(V.scalar_tensor_tensor(out=pb_, in0=pa, scalar=1.0 / 5, in1=q, op0=ALU.add, op1=ALU.mult))
    link(V.scalar_tensor_tensor(out=pa, in0=pb_, scalar=1.0 / 3, in1=q, op0=ALU.add, op1=ALU.mult))
    link(V.scalar_tensor_tensor(out=pb_, in0=pa, scalar=1.0, in1=s, op0=ALU.add, op1=ALU.mult))
    link(V.scalar_tensor_tensor(out=out, in0=pb_, scalar=2.0, in1=zmax, op0=ALU.mult, op1=ALU.add))


V_RSPLIT = 1 + 5 + 2 * KB * KB
V_LNVAR = V_RSPLIT + 8 + 6
V_AE = V_LNVAR + 4
V_AET = V_AE + 1
V_LMAX = V_AET + 1
V_SPLIT = V_LMAX + 7 + 5 * KB * G
V_DECAY = V_SPLIT + 1 + G + G + 1 + 13 + 4
V_XW = V_DECAY + W2R * NQ
V_LAYER = V_XW + KB
PE_X0 = 1
PE_AET = PE_X0 + KB + 1
PE_W1 = PE_AET
PE_H0 = PE_W1 + KB + 1
PE_W2 = PE_H0
PE_LAYER = PE_W2 + W2R
A_XT0 = 1
A_XR0 = A_XT0 + KB
A_SQRT = A_XR0 + 1
A_GELU = A_SQRT + KB
A_EXP0 = A_GELU + 2

_INS = ['x', 'cond_1024', 'L0_cond_Wx', 'L0_cond_Wh', 'L0_cond_b', 'L1_cond_conv_b', 'L1_cond_Wp', 'L1_cond_bp',
        'L1_cond_Ws', 'L1_cond_bs', 'L1_cond_A_log', 'L1_cond_dt_log', 'L1_cond_Wo', 'L1_cond_bo', 'L2_cond_Wx',
        'L2_cond_Wh', 'L2_cond_b', 'L3_cond_base_layer', 'L3_cond_w1', 'L3_cond_b1', 'L3_cond_w2', 'L3_cond_b2',
        'L3_cond_ln_g', 'L3_cond_ln_b']


def kernel(**inputs):
    import concourse.bacc as bacc
    from concourse.bass_utils import run_bass_kernel_spmd

    nc = bacc.Bacc("TRN2", target_bir_lowering=False, num_devices=1)
    arrays, args = {}, []
    for name in _INS:
        a = np.ascontiguousarray(inputs[name])
        arrays[f"in_{name}"] = a
        args.append(nc.dram_tensor(f"in_{name}", a.shape, mybir.dt.from_np(a.dtype), kind="ExternalInput").ap())
    out = nc.dram_tensor("out_0", (NB, T, D), F32, kind="ExternalOutput").ap()
    resid_stack_kernel(nc, *args, out)
    r = run_bass_kernel_spmd(nc, [arrays], core_ids=[0])
    return r.results[0]["out_0"]
```
